# Optimizing a Trainium2 kernel written in Bass

```python
import numpy as np
import jax
import jax.numpy as jnp

def _softmax(x, axis=-1):
    return jax.nn.softmax(x, axis=axis)

def _gelu(x):
    return jax.nn.gelu(x, approximate=True)

def _silu(x):
    return jax.nn.silu(x)

def _sigmoid(x):
    return jax.nn.sigmoid(x)

def _layernorm(x, axis=-1, eps=1e-05):
    m = jnp.mean(x, axis=axis, keepdims=True)
    v = jnp.var(x, axis=axis, keepdims=True)
    return (x - m) / jnp.sqrt(v + eps)

def _scatter_add(tgt, idx, src, axis=0):
    return tgt.at[idx].add(src)

def _segment_sum(src, seg, n):
    return jax.ops.segment_sum(src, seg, n)
kernel_name = 'mk_adj_seq_d2_adj_r2_a96eb5'

def setup_inputs(seed: int=0):
    np.random.seed(seed)
    _w = jnp.asarray

    def _rec_inputs():
        import jax
        import jax.numpy as jnp
        _gk = jax.random.key(seed)
        x = 7.22e-05 + 1 * jax.random.normal(jax.random.fold_in(_gk, 1), (128, 128, 256), jnp.float32)
        _a = jax.random.bernoulli(jax.random.fold_in(_gk, 2), 0.125, (128, 128, 128))
        _a = jnp.logical_or(_a, jnp.eye(128, dtype=bool))
        _af = _a.astype(jnp.float32)
        adj = _af
        return (x, adj)
    x, adj = _rec_inputs()

    def _L0_gnn_setup():
        import jax, jax.numpy as jnp
        import numpy as np
        BS, N, H = (8, 1024, 256)
        NEG_INF = -1000000000.0
        LEAKY_SLOPE = 0.01
        key = jax.random.key(seed)
        ks = jax.random.split(key, 8)
        feats = jax.random.normal(ks[0], (BS, N, H), dtype=jnp.float32)
        adj = jax.random.randint(ks[1], (BS, N, N), 0, 2).astype(jnp.float32)
        adj = jnp.maximum(adj, jnp.eye(N, dtype=jnp.float32)[None])
        s = 1.0 / np.sqrt(H)
        return {'feats': feats, 'adj_mat': adj, 'fc_w': jax.random.normal(ks[2], (H, H), dtype=jnp.float32) * s, 'fc_b': jax.random.normal(ks[3], (H,), dtype=jnp.float32) * s, 'q_w': jax.random.normal(ks[4], (1, H), dtype=jnp.float32) * s, 'q_b': jax.random.normal(ks[5], (1,), dtype=jnp.float32) * s, 'k_w': jax.random.normal(ks[6], (1, H), dtype=jnp.float32) * s, 'k_b': jax.random.normal(ks[7], (1,), dtype=jnp.float32) * s}
    _L0_gnn_all = _L0_gnn_setup()
    _L0_gnn_in = {k: v for k, v in _L0_gnn_all.items() if k in ('fc_w', 'fc_b', 'q_w', 'q_b', 'k_w', 'k_b')}
    del _L0_gnn_all

    def _L1_gnn_setup():
        import jax, jax.numpy as jnp
        import numpy as np
        B, N, D, H = (8, 512, 256, 8)
        DK = D // H
        LN_EPS = 1e-05
        ADJ_MIN = 1e-08

        def _layer_norm(x, gamma, beta):
            mu = jnp.mean(x, axis=-1, keepdims=True)
            var = jnp.mean(jnp.square(x - mu), axis=-1, keepdims=True)
            return (x - mu) * jax.lax.rsqrt(var + LN_EPS) * gamma + beta
        key = jax.random.key(seed)
        ks = jax.random.split(key, 12)
        x = jax.random.normal(ks[0], (B, N, D), dtype=jnp.float32)
        adj = jax.random.uniform(ks[1], (B, N, N), dtype=jnp.float32)
        adj = adj / jnp.sum(adj, axis=-1, keepdims=True)
        s = 1.0 / np.sqrt(D)
        Wq = jax.random.normal(ks[2], (D, D), dtype=jnp.float32) * s
        bq = jnp.zeros((D,), dtype=jnp.float32)
        Wk = jax.random.normal(ks[3], (D, D), dtype=jnp.float32) * s
        bk = jnp.zeros((D,), dtype=jnp.float32)
        Wv = jax.random.normal(ks[4], (D, D), dtype=jnp.float32) * s
        bv = jnp.zeros((D,), dtype=jnp.float32)
        Wo = jax.random.normal(ks[5], (D, D), dtype=jnp.float32) * s
        bo = jnp.zeros((D,), dtype=jnp.float32)
        gamma = jnp.ones((D,), dtype=jnp.float32)
        beta = jnp.zeros((D,), dtype=jnp.float32)
        return {'x': x, 'adj': adj, 'Wq': Wq, 'bq': bq, 'Wk': Wk, 'bk': bk, 'Wv': Wv, 'bv': bv, 'Wo': Wo, 'bo': bo, 'gamma': gamma, 'beta': beta}
    _L1_gnn_all = _L1_gnn_setup()
    _L1_gnn_in = {k: v for k, v in _L1_gnn_all.items() if k in ('Wq', 'bq', 'Wk', 'bk', 'Wv', 'bv', 'Wo', 'bo', 'gamma', 'beta')}
    del _L1_gnn_all
    return {'x': x, 'adj': adj, 'L0_gnn_fc_w': _L0_gnn_in['fc_w'], 'L0_gnn_fc_b': _L0_gnn_in['fc_b'], 'L0_gnn_q_w': _L0_gnn_in['q_w'], 'L0_gnn_q_b': _L0_gnn_in['q_b'], 'L0_gnn_k_w': _L0_gnn_in['k_w'], 'L0_gnn_k_b': _L0_gnn_in['k_b'], 'L1_gnn_Wq': _L1_gnn_in['Wq'], 'L1_gnn_bq': _L1_gnn_in['bq'], 'L1_gnn_Wk': _L1_gnn_in['Wk'], 'L1_gnn_bk': _L1_gnn_in['bk'], 'L1_gnn_Wv': _L1_gnn_in['Wv'], 'L1_gnn_bv': _L1_gnn_in['bv'], 'L1_gnn_Wo': _L1_gnn_in['Wo'], 'L1_gnn_bo': _L1_gnn_in['bo'], 'L1_gnn_gamma': _L1_gnn_in['gamma'], 'L1_gnn_beta': _L1_gnn_in['beta']}

def reference(x, adj, L0_gnn_fc_w, L0_gnn_fc_b, L0_gnn_q_w, L0_gnn_q_b, L0_gnn_k_w, L0_gnn_k_b, L1_gnn_Wq, L1_gnn_bq, L1_gnn_Wk, L1_gnn_bk, L1_gnn_Wv, L1_gnn_bv, L1_gnn_Wo, L1_gnn_bo, L1_gnn_gamma, L1_gnn_beta):
    import jax
    import jax.numpy as jnp

    def _L0_gnn_ref(feats, adj_mat, fc_w, fc_b, q_w, q_b, k_w, k_b):
        import jax, jax.numpy as jnp
        import numpy as np
        BS, N, H = (8, 1024, 256)
        NEG_INF = -1000000000.0
        LEAKY_SLOPE = 0.01
        feat_proj = jnp.einsum('bnh,oh->bno', feats, fc_w) + fc_b
        q = jnp.einsum('bnh,oh->bno', feat_proj, q_w) + q_b
        k = jnp.einsum('bnh,oh->bno', feat_proj, k_w) + k_b
        logits = q + jnp.swapaxes(k, 2, 1)
        masked = logits + (1.0 - adj_mat) * NEG_INF
        masked = jnp.where(masked >= 0, masked, LEAKY_SLOPE * masked)
        atten = jax.nn.softmax(masked, axis=-1)
        out = jnp.einsum('bnm,bmh->bnh', atten, feat_proj)
        return out + feats

    def _L1_gnn_ref(x, adj, Wq, bq, Wk, bk, Wv, bv, Wo, bo, gamma, beta):
        import jax, jax.numpy as jnp
        import numpy as np
        B, N, D, H = (8, 512, 256, 8)
        DK = D // H
        LN_EPS = 1e-05
        ADJ_MIN = 1e-08

        def _layer_norm(x, gamma, beta):
            mu = jnp.mean(x, axis=-1, keepdims=True)
            var = jnp.mean(jnp.square(x - mu), axis=-1, keepdims=True)
            return (x - mu) * jax.lax.rsqrt(var + LN_EPS) * gamma + beta
        b, n, d = x.shape
        q = (x @ Wq.T + bq).reshape(b, n, H, DK).transpose(0, 2, 1, 3)
        k = (x @ Wk.T + bk).reshape(b, n, H, DK).transpose(0, 2, 1, 3)
        v = (x @ Wv.T + bv).reshape(b, n, H, DK).transpose(0, 2, 1, 3)
        logits = jnp.einsum('bhqd,bhkd->bhqk', q, k) / np.sqrt(DK)
        logits = logits + jnp.log(jnp.clip(adj, ADJ_MIN, None))[:, None, :, :]
        attn = jax.nn.softmax(logits, axis=-1)
        out = jnp.einsum('bhqk,bhkd->bhqd', attn, v)
        out = out.transpose(0, 2, 1, 3).reshape(b, n, d)
        out = out @ Wo.T + bo
        return _layer_norm(x + out, gamma, beta)
    x = _L0_gnn_ref(x, adj, L0_gnn_fc_w, L0_gnn_fc_b, L0_gnn_q_w, L0_gnn_q_b, L0_gnn_k_w, L0_gnn_k_b)
    x = _L1_gnn_ref(x, adj, L1_gnn_Wq, L1_gnn_bq, L1_gnn_Wk, L1_gnn_bk, L1_gnn_Wv, L1_gnn_bv, L1_gnn_Wo, L1_gnn_bo, L1_gnn_gamma, L1_gnn_beta)
    return x

_drawn_inputs = setup_inputs


def setup_inputs(seed=0):
    import zlib

    import numpy as np

    out = dict(_drawn_inputs(seed))
    spreads = {'L1_gnn_bq': (0.0, 0.274),
     'L1_gnn_bk': (0.0, 0.8),
     'L1_gnn_bv': (0.0, 0.1),
     'L1_gnn_bo': (0.0, 0.1),
     'L1_gnn_gamma': (1.0, 0.2),
     'L1_gnn_beta': (0.0, 0.1)}
    factors = {}
    for name, (base, spread) in spreads.items():
        noise = np.random.default_rng([zlib.crc32(name.encode()), seed]).standard_normal(out[name].shape)
        drawn = base * np.exp(spread * noise) if base else spread * noise
        out[name] = jnp.asarray(drawn.astype(out[name].dtype))
    for name, factor in factors.items():
        out[name] = (out[name] * factor).astype(out[name].dtype)
    return out
```

```python
from contextlib import ExitStack

import concourse.bass as bass
from concourse import mybir

B, N, D = 128, 128, 256
H = 8
DK = D // H
P = 128
C = D // P
HC = H // C
G = 4
T = B // G
NEG = -1.0e9
SLOPE = 0.01
CLIP = 1e-8
EPS = 1e-5
SCALE = float(DK) ** -0.5

F32 = mybir.dt.float32
ALU = mybir.AluOpType
ACT = mybir.ActivationFunctionType
AX_X = mybir.AxisListType.X

FRONT0 = ["V01", "fp1", "fp3", "V23", "AV01", "x1T01", "Q0", "K0"]
FRONT1 = ["fp0", "fp2", "kb", "ET", "AV23", "x1T23", "Q1", "K1"]
NEXT0 = [n for n in FRONT0 if n[0] != "V"]
OWN0 = [n for n in FRONT0 if n[0] == "V"]


def gat_then_attention(nc, x, xT, adj, fc_w, fc_wT, fc_b, q_w, q_b, k_w, k_b,
                       WqT, bq, WkT, bk, WvT, bv, WoT, bo, gamma, beta, out):
    with ExitStack() as ctx:
        def sb(name, *shape):
            return ctx.enter_context(nc.sbuf_tensor(name, [P, *shape], F32))

        def bank(name):
            return ctx.enter_context(nc.psum_tensor(name, [P, 512], F32))

        def sem(name):
            return ctx.enter_context(nc.semaphore(name))

        ident = sb("ident", P)
        ones = sb("ones", P)
        halves = sb("halves", 1)
        fcw_nat = sb("fcw_nat", C, D)
        fcw = sb("fcw", C, D + 2)
        qk_w = sb("qk_w", C, 2)
        fcb_col = sb("fcb_col", C)
        qkb = sb("qkb", 2)
        fcb = sb("fcb", D + 2)
        wq, wk, wv, wo = (sb(n, C, D) for n in ("wq", "wk", "wv", "wo"))
        bq_col, bk_col, bv_col = (sb(n, C) for n in ("bq_col", "bk_col", "bv_col"))
        bq_scaled = sb("bq_scaled", C)
        bo_row, gamma_row, beta_row = (sb(n, D) for n in ("bo_row", "gamma_row", "beta_row"))
        x_in = sb("x_in", G, D)
        xT_in = sb("xT_in", G, C, N)
        adj_in = sb("adj_in", G, N)
        mask = sb("mask", G, N)
        fp = sb("fp", G, D + 2)
        logit = sb("logit", G, N)
        leaky = sb("leaky", G, N)
        neg_max0 = sb("neg_max0", G)
        neg_leaky_max = sb("neg_leaky_max", G)
        exp0 = sb("exp0", G, N)
        sum0 = sb("sum0", G)
        rinv0 = sb("rinv0", G)
        exp0T = sb("exp0T", G, N)
        x1 = sb("x1", G, D)
        x1T = sb("x1T", G, C, N)
        resid = sb("resid", G, D)
        adj_clip = sb("adj_clip", G, N)
        QT = sb("QT", C, G, N)
        KT = sb("KT", C, G, HC, N)
        V = sb("V", G, D)
        neg_max = sb("neg_max", H)
        probs = sb("probs", 2, H, N)
        sums = sb("sums", H)
        rinv = sb("rinv", H)
        probsT = sb("probsT", H, N)
        OT = sb("OT", C, N)
        y = sb("y", D)
        stats = sb("stats", 6)
        mean_var = sb("mean_var", 2)
        var_eps = sb("var_eps", 1)
        rstd = sb("rstd", 1)
        centred = sb("centred", D)
        out_sb = sb("out_sb", G, D)

        s_ps = [bank("s_ps0"), bank("s_ps1")]
        pt_ps = [bank("pt_ps0"), bank("pt_ps1")]
        f_ps = [bank("f_ps0"), bank("f_ps1")]
        ot_ps = bank("ot_ps")
        y_ps = bank("y_ps")

        weights_loaded = sem("weights_loaded")
        ident_step = sem("ident_step")
        consts_ready = sem("consts_ready")
        kt_zeroed = sem("kt_zeroed")
        fold_filled = sem("fold_filled")
        fold_copied = sem("fold_copied")
        bias_step = sem("bias_step")
        bq_ready = sem("bq_ready")
        x_loaded, xT_loaded, adj_loaded = sem("x_loaded"), sem("xT_loaded"), sem("adj_loaded")
        f_filled = [sem("f_filled0"), sem("f_filled1")]
        f_drained = [sem("f_drained0"), sem("f_drained1")]
        mask_ready = sem("mask_ready")
        leaky_ready = sem("leaky_ready")
        max0_ready = sem("max0_ready")
        neg_leaky_ready = sem("neg_leaky_ready")
        exp0_ready = sem("exp0_ready")
        rinv0_ready = sem("rinv0_ready")
        resid_ready = sem("resid_ready")
        clip_ready = sem("clip_ready")
        kt_ready = sem("kt_ready")
        s_filled = [sem("s_filled0"), sem("s_filled1")]
        max_ready = [sem("max_ready0"), sem("max_ready1")]
        exp_ready = [sem("exp_ready0"), sem("exp_ready1")]
        masked_ready = [sem("masked_ready0"), sem("masked_ready1")]
        sum_ready = [sem("sum_ready0"), sem("sum_ready1")]
        rinv_ready = [sem("rinv_ready0"), sem("rinv_ready1")]
        probs_ready = [sem("probs_ready0"), sem("probs_ready1")]
        pt_filled = [sem("pt_filled0"), sem("pt_filled1")]
        pt_copied = [sem("pt_copied0"), sem("pt_copied1")]
        ot_filled, ot_copied = sem("ot_filled"), sem("ot_copied")
        y_filled, y_ready = sem("y_filled"), sem("y_ready")
        stats_ready, var_ready = sem("stats_ready"), sem("var_ready")
        eps_added, rstd_ready = sem("eps_added"), sem("rstd_ready")
        centred_ready, out_ready = sem("centred_ready"), sem("out_ready")
        out_stored = [sem(f"out_stored{s}") for s in range(G)]

        x_g = x.rearrange("(t g) n d -> t n g d", g=G)
        xT_g = xT.rearrange("(t g) (c p) n -> t p g c n", g=G, p=P)
        adj_g = adj.rearrange("(t g) n m -> t n g m", g=G)
        out_g = out.rearrange("(t g) n d -> t g n d", g=G)

        def at_least(eng, semaphore, value):
            if not (isinstance(value, int) and value <= 0):
                eng.wait_ge(semaphore, value)

        def wait_apart(eng, semaphore, value):
            eng.wait_ge(weights_loaded, 16 * len(WEIGHTS))
            eng.wait_ge(semaphore, value)

        def use0(name, t, front, attn):
            order = FRONT0 if front and attn else NEXT0 if front else OWN0
            return (0 if isinstance(t, int) and t < 0 else len(NEXT0) + len(FRONT0) * t) + order.index(name)

        def use1(name, t):
            return len(FRONT1) * (t + 1) + FRONT1.index(name)

        def over_groups(eng, iteration):
            iteration(-1, True, False)
            iteration(0, True, True)
            with eng.Fori(1, T - 1) as t:
                iteration(t, True, True)
            iteration(T - 1, False, True)

        WEIGHTS = [
            (fcw_nat[:, :, :], fc_w.rearrange("(c p) n -> p c n", p=P)),
            (fcw[:, :, 0:D], fc_wT.rearrange("(c p) n -> p c n", p=P)),
            (wq[:, :, :], WqT.rearrange("(c p) n -> p c n", p=P)),
            (wk[:, :, :], WkT.rearrange("(c p) n -> p c n", p=P)),
            (wv[:, :, :], WvT.rearrange("(c p) n -> p c n", p=P)),
            (wo[:, :, :], WoT.rearrange("(c p) n -> p c n", p=P)),
            (qk_w[:, :, 0], q_w.rearrange("a (c p) -> p (a c)", p=P)),
            (qk_w[:, :, 1], k_w.rearrange("a (c p) -> p (a c)", p=P)),
            (fcb_col[:, :], fc_b.rearrange("(c p) -> p c", p=P)),
            (bq_col[:, :], bq.rearrange("(c p) -> p c", p=P)),
            (bk_col[:, :], bk.rearrange("(c p) -> p c", p=P)),
            (bv_col[:, :], bv.rearrange("(c p) -> p c", p=P)),
            (fcb[:, 0:D], fc_b.partition_broadcast(P)),
            (bo_row[:, :], bo.partition_broadcast(P)),
            (gamma_row[:, :], gamma.partition_broadcast(P)),
            (beta_row[:, :], beta.partition_broadcast(P)),
            (qkb[:, 0:1], q_b.partition_broadcast(P)),
            (qkb[:, 1:2], k_b.partition_broadcast(P)),
        ]

        block = ctx.enter_context(nc.Block())

        @block.sync
        def _(sp):
            for dst, src in WEIGHTS:
                sp.dma_start(dst, src, allow_slow_non_contiguous=True).then_inc(weights_loaded, 16)

            def load_xT(u):
                if isinstance(u, int) and u == 1:
                    sp.wait_ge(f_filled[0], NEXT0.index("fp3") + 1)
                elif not isinstance(u, int) or u > 1:
                    sp.wait_ge(f_filled[0], use0("fp3", u - 2, True, True) + 1)
                sp.dma_start(xT_in[:, :, :, :], xT_g[u]).then_inc(xT_loaded, 16)

            def load_x(u):
                if not (isinstance(u, int) and u == 0):
                    sp.wait_ge(f_drained[1], use1("AV23", u - 2) + 1)
                sp.dma_start(x_in[:, :, :], x_g[u]).then_inc(x_loaded, 16)

            def load_adj(u):
                at_least(sp, clip_ready, u)
                sp.dma_start(adj_in[:, :, :], adj_g[u]).then_inc(adj_loaded, 16)

            def store(t, s):
                sp.wait_ge(out_ready, G * t + s + 1)
                sp.dma_start(out_g[t, s], out_sb[:, s, :]).then_inc(out_stored[s], 16)

            def iteration(t, load, attn):
                if load:
                    load_xT(t + 2)
                if attn:
                    store(t, 0)
                if load:
                    load_x(t + 2)
                if attn:
                    store(t, 1)
                    store(t, 2)
                if load:
                    load_adj(t + 2)
                if attn:
                    store(t, 3)

            load_xT(0)
            load_x(0)
            load_adj(0)
            iteration(-1, True, False)
            iteration(0, True, True)
            with sp.Fori(1, T - 2) as t:
                iteration(t, True, True)
            iteration(T - 2, False, True)
            iteration(T - 1, False, True)
            for s in range(G):
                sp.wait_ge(out_stored[s], 16 * T)

        @block.tensor
        def _(pe):
            mm, tr = nc.tensor.matmul, nc.tensor.transpose
            pe.wait_ge(weights_loaded, 16 * len(WEIGHTS))
            pe.wait_ge(consts_ready, 1)
            for c in range(C):
                for o in range(C):
                    mm(y_ps[:, 2 * c:2 * c + 2], fcw_nat[:, o, c * P:(c + 1) * P], qk_w[:, o, :],
                       start=(o == 0), stop=(o == C - 1))
            for o in range(C):
                last = mm(y_ps[:, 4:6], fcb_col[:, o:o + 1].to_broadcast([P, P]), qk_w[:, o, :],
                          start=(o == 0), stop=(o == C - 1))
            last.then_inc(fold_filled, 1)
            pe.wait_ge(fold_copied, 2)

            def iteration(t, front, attn):
                u = t + 1

                def fill0(name):
                    at_least(pe, f_drained[0], use0(name, t, front, attn))
                    if name == "V01":
                        pe.wait_ge(kt_ready, C * t + 1)

                def fill1(name):
                    at_least(pe, f_drained[1], use1(name, t))
                    if name == "fp0":
                        at_least(pe, kt_ready, C * (t + 1))

                def projected(g):
                    b = 1 - g % 2
                    (fill1 if b else fill0)(f"fp{g}")
                    for c in range(C):
                        last = mm(f_ps[b][:, 0:D + 2], xT_in[:, g, c, :], fcw[:, c, :],
                                  start=(c == 0), stop=(c == C - 1))
                    last.then_inc(f_filled[b], 1)

                def values(name, g0):
                    fill0(name)
                    for g in (g0, g0 + 1):
                        for c in range(C):
                            last = mm(f_ps[0][:, (g - g0) * D:(g - g0 + 1) * D], x1T[:, g, c, :], wv[:, c, :],
                                      start=(c == 0), stop=(c == C - 1))
                    last.then_inc(f_filled[0], 1)

                def scores(s):
                    n = G * t + s
                    for h2 in range(C):
                        at_least(pe, exp_ready[h2], n)
                        mm(s_ps[h2][:, :], QT[:, h2, s, :], KT[:, h2, s, :, :],
                           start=True, stop=True).then_inc(s_filled[h2], 1)

                def transpose_probs(s):
                    n = G * t + s
                    for h2 in range(C):
                        at_least(pe, pt_copied[h2], n)
                        pe.wait_ge(probs_ready[h2], n + 1)
                        for h in range(HC):
                            last = tr(pt_ps[h2][:, h * N:(h + 1) * N], probs[:, s % 2, h2 * HC + h, :], ident[:, :])
                        last.then_inc(pt_filled[h2], 1)

                def attend(s):
                    n = G * t + s
                    at_least(pe, ot_copied, n)
                    if s == 0:
                        pe.wait_ge(f_drained[0], use0("V01", t, front, attn) + 1)
                    if s == 2:
                        pe.wait_ge(f_drained[0], use0("V23", t, front, attn) + 1)
                    for h2 in range(C):
                        pe.wait_ge(pt_copied[h2], n + 1)
                        for h in range(HC):
                            f0 = (h2 * HC + h) * DK
                            last = mm(ot_ps[h * DK:(h + 1) * DK, h2 * N:(h2 + 1) * N], V[:, s, f0:f0 + DK],
                                      probsT[:, h2 * HC + h, :], start=True, stop=True)
                    last.then_inc(ot_filled, 1)

                def project_out(s):
                    n = G * t + s
                    at_least(pe, y_ready, n)
                    pe.wait_ge(ot_copied, n + 1)
                    for c in range(C):
                        last = mm(y_ps[:, 0:D], OT[:, c, :], wo[:, c, :], start=(c == 0), stop=(c == C - 1))
                    last.then_inc(y_filled, 1)

                def aggregate(g0):
                    b = g0 // 2
                    (fill1 if b else fill0)("AV23" if b else "AV01")
                    for g in (g0, g0 + 1):
                        last = mm(f_ps[b][:, (g - g0) * D:(g - g0 + 1) * D], exp0T[:, g, :], fp[:, g, 0:D],
                                  start=True, stop=True)
                    last.then_inc(f_filled[b], 1)

                def broadcast_k():
                    fill1("kb")
                    pe.wait_ge(f_drained[0], use0("fp3", t, front, attn) + 1)
                    for g in range(G):
                        last = mm(f_ps[1][:, g * N:(g + 1) * N], fp[:, g, D + 1:D + 2].to_broadcast([P, P]),
                                  ident[:, :], start=True, stop=True)
                    last.then_inc(f_filled[1], 1)

                def transpose_exp0():
                    fill1("ET")
                    for g in range(G):
                        pe.wait_ge(exp0_ready, G * u + g + 1)
                        last = tr(f_ps[1][:, g * N:(g + 1) * N], exp0[:, g, :], ident[:, :])
                    last.then_inc(f_filled[1], 1)

                def transpose_x1(g0):
                    b = g0 // 2
                    (fill1 if b else fill0)("x1T23" if b else "x1T01")
                    for g in (g0, g0 + 1):
                        for c in range(C):
                            last = tr(f_ps[b][:, ((g - g0) * C + c) * N:((g - g0) * C + c + 1) * N],
                                      x1[:, g, c * P:(c + 1) * P], ident[:, :])
                    last.then_inc(f_filled[b], 1)

                def project(name, w, o):
                    (fill1 if o else fill0)(name)
                    for c in range(C):
                        last = mm(f_ps[o][:, :], w[:, c, o * P:(o + 1) * P], x1T[:, :, c, :],
                                  start=(c == 0), stop=(c == C - 1))
                    last.then_inc(f_filled[o], 1)

                if attn:
                    values("V01", 0)
                    pe.wait_ge(f_drained[1], use1("fp0", t))
                    pe.wait_ge(kt_ready, C * (t + 1))
                    scores(0)
                if front:
                    pe.wait_ge(xT_loaded, 16 * (u + 1))
                    for g in range(G):
                        projected(g)
                if attn:
                    scores(1)
                if front:
                    broadcast_k()
                if attn:
                    values("V23", 2)
                    transpose_probs(0)
                    scores(2)
                    attend(0)
                if front:
                    transpose_exp0()
                if attn:
                    project_out(0)
                    transpose_probs(1)
                if front:
                    pe.wait_ge(f_drained[1], use1("ET", t) + 1)
                    aggregate(0)
                if attn:
                    attend(1)
                    scores(3)
                if front:
                    aggregate(2)
                if attn:
                    transpose_probs(2)
                if front:
                    transpose_x1(0)
                    transpose_x1(2)
                if attn:
                    project_out(1)
                    attend(2)
                if front:
                    pe.wait_ge(f_drained[0], use0("x1T01", t, front, attn) + 1)
                    pe.wait_ge(f_drained[1], use1("x1T23", t) + 1)
                    project("Q0", wq, 0)
                    project("Q1", wq, 1)
                if attn:
                    transpose_probs(3)
                    project_out(2)
                if front:
                    project("K0", wk, 0)
                if attn:
                    attend(3)
                if front:
                    project("K1", wk, 1)
                if attn:
                    project_out(3)

            over_groups(pe, iteration)

        @block.scalar
        def _(act):
            fn = nc.scalar.activation

            def iteration(t, front, attn):
                u = t + 1

                def exp_half(s, h2):
                    act.wait_ge(max_ready[h2], G * t + s + 1)
                    for h in range(HC):
                        last = fn(probs[:, s % 2, h2 * HC + h, :], s_ps[h2][:, h * N:(h + 1) * N], ACT.Exp,
                                  bias=neg_max[:, h2 * HC + h:h2 * HC + h + 1])
                    last.then_inc(exp_ready[h2], 1)

                def copy_pt(s):
                    act.wait_ge(pt_filled[0], G * t + s + 1)
                    fn(probsT[:, 0:HC, :], pt_ps[0][:, :], ACT.Copy).then_inc(pt_copied[0], 1)

                def copy_ot(s):
                    act.wait_ge(ot_filled, G * t + s + 1)
                    for c in range(C):
                        last = fn(OT[:, c, :], ot_ps[:, c * N:(c + 1) * N], ACT.Identity, bias=bv_col[:, c:c + 1])
                    last.then_inc(ot_copied, 1)

                def copy_v(name, g0):
                    act.wait_ge(f_filled[0], use0(name, t, front, attn) + 1)
                    fn(V[:, g0:g0 + 2, :], f_ps[0][:, :], ACT.Copy).then_inc(f_drained[0], 1)

                def copy_q(o):
                    act.wait_ge(f_filled[o], (use1("Q1", t) if o else use0("Q0", t, front, attn)) + 1)
                    fn(QT[:, o, :, :], f_ps[o][:, :], ACT.Identity, bias=bq_scaled[:, o:o + 1],
                       scale=SCALE).then_inc(f_drained[o], 1)

                def copy_k(o):
                    act.wait_ge(f_filled[o], (use1("K1", t) if o else use0("K0", t, front, attn)) + 1)
                    for h in range(HC // 2):
                        q = slice(h * DK, (h + 1) * DK)
                        last = fn(KT[q, o, :, h, :], f_ps[o][q, :], ACT.Identity, bias=bk_col[q, o:o + 1])
                    last.then_inc(f_drained[o], 1)

                def exp_first_layer():
                    act.wait_ge(leaky_ready, u + 1)
                    act.wait_ge(neg_leaky_ready, u + 1)
                    for g in range(G):
                        fn(exp0[:, g, :], leaky[:, g, :], ACT.Exp, bias=neg_leaky_max[:, g:g + 1],
                           accum_out=sum0[:, g:g + 1]).then_inc(exp0_ready, 1)

                def copy_exp0T():
                    act.wait_ge(f_filled[1], use1("ET", t) + 1)
                    fn(exp0T[:, :, :], f_ps[1][:, :], ACT.Copy).then_inc(f_drained[1], 1)

                def copy_x1T():
                    act.wait_ge(f_filled[0], use0("x1T01", t, front, attn) + 1)
                    fn(x1T[:, 0:2, :, :], f_ps[0][:, :], ACT.Copy).then_inc(f_drained[0], 1)
                    act.wait_ge(f_filled[1], use1("x1T23", t) + 1)
                    fn(x1T[:, 2:4, :, :], f_ps[1][:, :], ACT.Copy).then_inc(f_drained[1], 1)

                if attn:
                    copy_v("V01", 0)
                    exp_half(0, 0)
                    exp_half(0, 1)
                    exp_half(1, 0)
                    exp_half(1, 1)
                    copy_v("V23", 2)
                    copy_pt(0)
                if front:
                    exp_first_layer()
                if attn:
                    copy_ot(0)
                if front:
                    copy_exp0T()
                if attn:
                    exp_half(2, 0)
                    copy_pt(1)
                    exp_half(2, 1)
                    copy_ot(1)
                    exp_half(3, 0)
                    exp_half(3, 1)
                    copy_pt(2)
                if front:
                    copy_x1T()
                if attn:
                    copy_ot(2)
                if front:
                    copy_q(0)
                    copy_q(1)
                if attn:
                    copy_pt(3)
                if front:
                    copy_k(0)
                if attn:
                    copy_ot(3)
                if front:
                    copy_k(1)

            act.wait_ge(weights_loaded, 16 * len(WEIGHTS))
            fn(bq_scaled[:, :], bq_col[:, :], ACT.Copy, scale=SCALE).then_inc(bq_ready, 1)
            act.wait_ge(bq_ready, 1)
            act.wait_ge(kt_zeroed, 1)
            over_groups(act, iteration)

        @block.vector
        def _(dve):
            v = nc.vector

            def iteration(t, front, attn):
                u = t + 1

                def row_max(s):
                    for h2 in range(C):
                        dve.wait_ge(s_filled[h2], G * t + s + 1)
                        v.tensor_reduce(neg_max[:, h2 * HC:(h2 + 1) * HC],
                                        s_ps[h2][:, :].rearrange("p (h n) -> p h n", h=HC), AX_X, ALU.max,
                                        negate=True).then_inc(max_ready[h2], 1)

                def row_sum(s, h2):
                    n = G * t + s
                    hs = slice(h2 * HC, (h2 + 1) * HC)
                    dve.wait_ge(masked_ready[h2], n + 1)
                    v.tensor_reduce(sums[:, hs], probs[:, s % 2, hs, :], AX_X, ALU.add).then_inc(sum_ready[h2], 1)
                    dve.wait_ge(sum_ready[h2], n + 1)
                    v.reciprocal(rinv[:, hs], sums[:, hs]).then_inc(rinv_ready[h2], 1)

                def copy_pt(s):
                    dve.wait_ge(pt_filled[1], G * t + s + 1)
                    v.tensor_copy(probsT[:, HC:H, :],
                                  pt_ps[1][:, :].rearrange("p (h n) -> p h n", h=HC)).then_inc(pt_copied[1], 1)

                def project_drain(g):
                    b = 1 - g % 2
                    name = f"fp{g}"
                    dve.wait_ge(f_filled[b], (use1(name, t) if b else use0(name, t, front, attn)) + 1)
                    v.tensor_tensor(fp[:, g, :], f_ps[b][:, 0:D + 2], fcb[:, :], ALU.add).then_inc(f_drained[b], 1)

                def add_residual(s):
                    n = G * t + s
                    dve.wait_ge(y_filled, n + 1)
                    if s == 0:
                        dve.wait_ge(resid_ready, t + 1)
                    v.tensor_tensor(y[:, :], y_ps[:, 0:D], resid[:, s, :], ALU.add).then_inc(y_ready, 1)
                    dve.wait_ge(y_ready, n + 1)
                    v.bn_stats(stats[:, :], y[:, :]).then_inc(stats_ready, 1)
                    wait_apart(dve, stats_ready, n + 1)
                    at_least(dve, rstd_ready, n)
                    v.bn_aggr(mean_var[:, :], stats[:, :]).then_inc(var_ready, 1)

                def normalise(s):
                    n = G * t + s
                    dve.wait_ge(var_ready, n + 1)
                    v.scalar_tensor_tensor(centred[:, :], y[:, :], mean_var[:, 0:1], gamma_row[:, :],
                                           ALU.subtract, ALU.mult).then_inc(centred_ready, 1)
                    dve.wait_ge(centred_ready, n + 1)
                    dve.wait_ge(rstd_ready, n + 1)
                    at_least(dve, out_stored[s], 16 * t)
                    v.scalar_tensor_tensor(out_sb[:, s, :], centred[:, :], rstd[:, 0:1], beta_row[:, :],
                                           ALU.mult, ALU.add).then_inc(out_ready, 1)

                def first_layer(g0):
                    b = g0 // 2
                    dve.wait_ge(f_filled[b], (use1("AV23", t) if b else use0("AV01", t, front, attn)) + 1)
                    if g0 == 0:
                        dve.wait_ge(rinv0_ready, u + 1)
                        at_least(dve, resid_ready, u)
                        dve.wait_ge(x_loaded, 16 * (u + 1))
                    for g in (g0, g0 + 1):
                        last = v.scalar_tensor_tensor(x1[:, g, :], f_ps[b][:, (g - g0) * D:(g - g0 + 1) * D],
                                                      rinv0[:, g:g + 1], x_in[:, g, :], ALU.mult, ALU.add)
                    last.then_inc(f_drained[b], 1)

                def make_mask():
                    dve.wait_ge(adj_loaded, 16 * (u + 1))
                    v.tensor_scalar(mask[:, :, :], adj_in[:, :, :], 1.0, -NEG, ALU.subtract,
                                    ALU.mult).then_inc(mask_ready, 1)

                def clip_adj():
                    v.tensor_scalar(adj_clip[:, :, :], adj_in[:, :, :], CLIP, None, ALU.max).then_inc(clip_ready, 1)

                def first_softmax():
                    dve.wait_ge(f_filled[1], use1("kb", t) + 1)
                    dve.wait_ge(mask_ready, u + 1)
                    dve.wait_ge(f_drained[0], use0("fp3", t, front, attn) + 1)
                    dve.wait_ge(f_drained[1], use1("fp2", t) + 1)
                    for g in range(G):
                        last = v.scalar_tensor_tensor(logit[:, g, :], f_ps[1][:, g * N:(g + 1) * N],
                                                      fp[:, g, D:D + 1], mask[:, g, :], ALU.add, ALU.add)
                    last.then_inc(f_drained[1], 1)
                    dve.wait_ge(f_drained[1], use1("kb", t) + 1)
                    v.tensor_reduce(neg_max0[:, :], logit[:, :, :], AX_X, ALU.max, negate=True).then_inc(max0_ready, 1)
                    v.scalar_tensor_tensor(leaky[:, :, :], logit[:, :, :], SLOPE, logit[:, :, :],
                                           ALU.mult, ALU.max).then_inc(leaky_ready, 1)
                    dve.wait_ge(max0_ready, u + 1)
                    v.scalar_tensor_tensor(neg_leaky_max[:, :], neg_max0[:, :], SLOPE, neg_max0[:, :],
                                           ALU.mult, ALU.min).then_inc(neg_leaky_ready, 1)

                def invert_sum0():
                    dve.wait_ge(exp0_ready, G * (u + 1))
                    v.reciprocal(rinv0[:, :], sum0[:, :]).then_inc(rinv0_ready, 1)

                def copy_k(o):
                    dve.wait_ge(f_filled[o], (use1("K1", t) if o else use0("K0", t, front, attn)) + 1)
                    for h in range(HC // 2, HC):
                        q = slice(h * DK, (h + 1) * DK)
                        last = v.tensor_scalar(KT[q, o, :, h, :], f_ps[o][q, :].rearrange("p (g n) -> p g n", g=G),
                                               bk_col[q, o:o + 1], None, ALU.add)
                    last.then_inc(kt_ready, 1)

                if front:
                    make_mask()
                if attn:
                    row_max(0)
                if front:
                    project_drain(0)
                    project_drain(1)
                if attn:
                    row_sum(0, 0)
                if front:
                    project_drain(2)
                    project_drain(3)
                if attn:
                    row_sum(0, 1)
                    row_max(1)
                if front:
                    first_softmax()
                if attn:
                    row_sum(1, 0)
                    copy_pt(0)
                    row_sum(1, 1)
                    row_max(2)
                    add_residual(0)
                    copy_pt(1)
                    row_sum(2, 0)
                if front:
                    invert_sum0()
                    first_layer(0)
                if attn:
                    normalise(0)
                    row_sum(2, 1)
                    row_max(3)
                if front:
                    first_layer(2)
                if attn:
                    copy_pt(2)
                    row_sum(3, 0)
                    add_residual(1)
                    row_sum(3, 1)
                    normalise(1)
                if front:
                    clip_adj()
                if attn:
                    copy_pt(3)
                    add_residual(2)
                    normalise(2)
                if front:
                    copy_k(0)
                    copy_k(1)
                if attn:
                    add_residual(3)
                    normalise(3)

            v.memset(KT[:, :, :, :, :], 0.0).then_inc(kt_zeroed, 1)
            dve.wait_ge(weights_loaded, 16 * len(WEIGHTS))
            dve.wait_ge(fold_filled, 1)
            v.tensor_copy(fcw[:, :, D:D + 2],
                          y_ps[:, 0:4].rearrange("p (c w) -> p c w", c=C)).then_inc(fold_copied, 1)
            v.tensor_tensor(fcb[:, D:D + 2], y_ps[:, 4:6], qkb[:, :], ALU.add).then_inc(fold_copied, 1)
            dve.wait_ge(fold_copied, 2)
            over_groups(dve, iteration)

        @block.gpsimd
        def _(pool):
            g_ = nc.gpsimd

            def iteration(t, front, attn):
                u = t + 1

                def mask_probs(s):
                    for h2 in range(C):
                        hs = slice(h2 * HC, (h2 + 1) * HC)
                        pool.wait_ge(exp_ready[h2], G * t + s + 1)
                        g_.tensor_tensor(probs[:, s % 2, hs, :], probs[:, s % 2, hs, :],
                                         adj_clip[:, s:s + 1, :].to_broadcast([P, HC, N]),
                                         ALU.mult).then_inc(masked_ready[h2], 1)

                def scale_probs(s):
                    for h2 in range(C):
                        hs = slice(h2 * HC, (h2 + 1) * HC)
                        pool.wait_ge(rinv_ready[h2], G * t + s + 1)
                        g_.tensor_tensor(probs[:, s % 2, hs, :], probs[:, s % 2, hs, :],
                                         rinv[:, hs].unsqueeze(2).to_broadcast([P, HC, N]),
                                         ALU.mult).then_inc(probs_ready[h2], 1)

                def inverse_deviation(s):
                    n = G * t + s
                    wait_apart(pool, var_ready, n + 1)
                    g_.tensor_scalar(var_eps[:, :], mean_var[:, 1:2], EPS, None, ALU.add).then_inc(eps_added, 1)
                    pool.wait_ge(eps_added, n + 1)
                    at_least(pool, out_ready, n)
                    g_.tensor_tensor(rstd[:, :], var_eps[:, :], halves[:, :], ALU.pow).then_inc(rstd_ready, 1)

                if attn:
                    pool.wait_ge(f_drained[1], use1("AV23", t - 1) + 1)
                    g_.tensor_tensor(resid[:, :, :], x1[:, :, :],
                                     bo_row[:, :].unsqueeze(1).to_broadcast([P, G, D]),
                                     ALU.add).then_inc(resid_ready, 1)
                    pool.wait_ge(clip_ready, t + 1)
                    mask_probs(0)
                    scale_probs(0)
                    mask_probs(1)
                    scale_probs(1)
                    mask_probs(2)
                    inverse_deviation(0)
                    scale_probs(2)
                    mask_probs(3)
                    scale_probs(3)
                    inverse_deviation(1)
                    inverse_deviation(2)
                    inverse_deviation(3)

            g_.memset(ident[:, :], 0.0).then_inc(ident_step, 1)
            g_.memset(ones[:, :], 1.0)
            g_.memset(halves[:, :], -0.5).then_inc(ident_step, 1)
            pool.wait_ge(ident_step, 2)
            g_.affine_select(out=ident[:, :], in_=ident[:, :], compare_op=ALU.not_equal, fill=1.0, base=0,
                             pattern=[[-1, P]], channel_multiplier=1).then_inc(consts_ready, 1)
            pool.wait_ge(consts_ready, 1)
            pool.wait_ge(weights_loaded, 16 * len(WEIGHTS))
            over_groups(pool, iteration)


_INS = ["x", "xT", "adj", "fc_w", "fc_wT", "fc_b", "q_w", "q_b", "k_w", "k_b",
        "WqT", "bq", "WkT", "bk", "WvT", "bv", "WoT", "bo", "gamma", "beta"]


def kernel(x, adj, L0_gnn_fc_w, L0_gnn_fc_b, L0_gnn_q_w, L0_gnn_q_b, L0_gnn_k_w, L0_gnn_k_b,
           L1_gnn_Wq, L1_gnn_bq, L1_gnn_Wk, L1_gnn_bk, L1_gnn_Wv, L1_gnn_bv, L1_gnn_Wo, L1_gnn_bo,
           L1_gnn_gamma, L1_gnn_beta):
    import numpy as np
    import concourse.bacc as bacc
    from concourse.bass_utils import run_bass_kernel_spmd

    given = dict(
        x=x, xT=np.transpose(np.asarray(x), (0, 2, 1)), adj=adj,
        fc_w=L0_gnn_fc_w, fc_wT=np.asarray(L0_gnn_fc_w).T, fc_b=L0_gnn_fc_b,
        q_w=L0_gnn_q_w, q_b=L0_gnn_q_b, k_w=L0_gnn_k_w, k_b=L0_gnn_k_b,
        WqT=np.asarray(L1_gnn_Wq).T, bq=L1_gnn_bq, WkT=np.asarray(L1_gnn_Wk).T, bk=L1_gnn_bk,
        WvT=np.asarray(L1_gnn_Wv).T, bv=L1_gnn_bv, WoT=np.asarray(L1_gnn_Wo).T, bo=L1_gnn_bo,
        gamma=L1_gnn_gamma, beta=L1_gnn_beta,
    )
    nc = bacc.Bacc("TRN2", target_bir_lowering=False, num_devices=1)
    arrays, args = {}, []
    for name in _INS:
        a = np.ascontiguousarray(given[name])
        arrays[f"in_{name}"] = a
        args.append(nc.dram_tensor(f"in_{name}", a.shape, mybir.dt.from_np(a.dtype), kind="ExternalInput").ap())
    out = nc.dram_tensor("out", (B, N, D), F32, kind="ExternalOutput").ap()
    gat_then_attention(nc, *args, out)
    r = run_bass_kernel_spmd(nc, [arrays], core_ids=[0])
    return r.results[0]["out"]
```

```python
from contextlib import ExitStack

import concourse.bass as bass
from concourse import mybir

B, N, D = 128, 128, 256
H = 8
DK = D // H
P = 128
C = D // P
HC = H // C
G = 4
T = B // G
NEG = -1.0e9
SLOPE = 0.01
CLIP = 1e-8
EPS = 1e-5
SCALE = float(DK) ** -0.5

F32 = mybir.dt.float32
F32R = mybir.dt.float32r
ALU = mybir.AluOpType
ACT = mybir.ActivationFunctionType
AX_X = mybir.AxisListType.X

BANK_USES = [
    [("fp3", 1), ("fp0", 1), ("kb", 1), ("V1", 0), ("AV1", 1), ("xT1", 1), ("K1", 1), ("Q0", 1)],
    [("fp2", 1), ("fp1", 1), ("V0", 0), ("ET", 1), ("AV0", 1), ("xT0", 1), ("K0", 1), ("Q1", 1)],
]
WHERE = {name: (b, place, lead) for b, uses in enumerate(BANK_USES) for place, (name, lead) in enumerate(uses)}
LAST_FP, LAST_AV = "fp0", "AV1"


def gat_then_attention(nc, x, xT, adj, fc_w, fc_wT, fc_b, q_w, q_b, k_w, k_b,
                       WqT, bq, WkT, bk, WvT, bv, WoT, bo, gamma, beta, out):
    with ExitStack() as ctx:
        def sb(name, *shape):
            return ctx.enter_context(nc.sbuf_tensor(name, [P, *shape], F32))

        def halves_of(name, *shape):
            return tuple(ctx.enter_context(nc.sbuf_tensor(f"{name}_{part}", [P, *shape], F32R))
                         for part in ("hi", "lo"))

        def bank(name):
            return ctx.enter_context(nc.psum_tensor(name, [P, 512], F32))

        def sem(name):
            return ctx.enter_context(nc.semaphore(name))

        ident = sb("ident", P)
        halves = sb("halves", 1)
        eps_col = sb("eps_col", 1)
        fcw_nat = sb("fcw_nat", C, D)
        fcw = sb("fcw", C, D + 2)
        qk_w = sb("qk_w", C, 2)
        fcb_col = sb("fcb_col", C)
        qkb = sb("qkb", 2)
        logit_bias = sb("logit_bias", 1)
        fcb = sb("fcb", D)
        w_in = [sb(n, C, D) for n in ("wq_in", "wk_in", "wv_in", "wo_in")]
        wq, wk, wv, wo = (halves_of(n, C, D) for n in ("wq", "wk", "wv", "wo"))
        bq_col, bk_col, bv_col = (sb(n, C) for n in ("bq_col", "bk_col", "bv_col"))
        bq_scaled = sb("bq_scaled", C)
        bo_row, gamma_row, beta_row = (sb(n, D) for n in ("bo_row", "gamma_row", "beta_row"))
        x_in = sb("x_in", G, D)
        x_b = sb("x_b", G, D)
        xT_in = sb("xT_in", G, C, N)
        adj_in = sb("adj_in", G, N)
        mask = sb("mask", G, N)
        fp = sb("fp", G, D + 2)
        q_eff = sb("q_eff", G)
        logit = sb("logit", G, N)
        leaky = sb("leaky", G, N)
        neg_max0 = sb("neg_max0", G)
        neg_leaky_max = sb("neg_leaky_max", G)
        exp0 = sb("exp0", G, N)
        sum0 = sb("sum0", G)
        rinv0 = sb("rinv0", G)
        exp0T = sb("exp0T", G, N)
        x1 = sb("x1", G, D)
        x1T = halves_of("x1T", G, C, N)
        resid = sb("resid", G, D)
        adj_clip = sb("adj_clip", G, N)
        QT = halves_of("QT", C, G, N)
        KT = ctx.enter_context(nc.sbuf_tensor("KT", [P, C, 2, G, N], F32R))
        KD = ctx.enter_context(nc.sbuf_tensor("KD", [P, C, HC, 2, G, N], F32R))
        V = sb("V", G, D)
        neg_max = sb("neg_max", H)
        probs = sb("probs", 2, H, N)
        sums = sb("sums", 2, H)
        rinv = sb("rinv", 2, H)
        probsT = sb("probsT", H, N)
        OT = halves_of("OT", C, N)
        y = sb("y", 2, D)
        stats = sb("stats", 6)
        mean_var = sb("mean_var", 2, 2)
        var_eps = sb("var_eps", 2, 1)
        rstd = sb("rstd", 2, 1)
        centred = sb("centred", 2, D)
        out_sb = sb("out_sb", G, D)

        s_ps = [bank("s_ps0"), bank("s_ps1")]
        pt_ps = [bank("pt_ps0"), bank("pt_ps1")]
        f_ps = [bank("f_ps0"), bank("f_ps1")]
        ot_ps = bank("ot_ps")
        y_ps = bank("y_ps")

        weights_loaded = sem("weights_loaded")
        ident_step = sem("ident_step")
        consts_ready = sem("consts_ready")
        kd_zeroed = sem("kd_zeroed")
        fold_filled = sem("fold_filled")
        fold_copied = sem("fold_copied")
        weights_hi, weights_split = sem("weights_hi"), sem("weights_split")
        x_loaded, xT_loaded, adj_loaded = sem("x_loaded"), sem("xT_loaded"), sem("adj_loaded")
        f_filled = [sem("f_filled0"), sem("f_filled1")]
        f_drained = [sem("f_drained0"), sem("f_drained1")]
        mask_ready = sem("mask_ready")
        leaky_ready = sem("leaky_ready")
        max0_ready = sem("max0_ready")
        neg_leaky_ready = sem("neg_leaky_ready")
        exp0_ready = sem("exp0_ready")
        rinv0_ready = sem("rinv0_ready")
        resid_ready = sem("resid_ready")
        clip_ready = sem("clip_ready")
        x_b_ready = sem("x_b_ready")
        q_eff_ready = sem("q_eff_ready")
        x1T_hi_ready = [sem("x1T_hi_ready0"), sem("x1T_hi_ready1")]
        k_hi_ready = [sem("k_hi_ready0"), sem("k_hi_ready1")]
        q_hi_ready = [sem("q_hi_ready0"), sem("q_hi_ready1")]
        kd_spread = [sem("kd_spread0"), sem("kd_spread1")]
        s_filled = [sem("s_filled0"), sem("s_filled1")]
        max_ready = [sem("max_ready0"), sem("max_ready1")]
        exp_ready = [sem("exp_ready0"), sem("exp_ready1")]
        masked_ready = [sem("masked_ready0"), sem("masked_ready1")]
        sum_ready = [sem("sum_ready0"), sem("sum_ready1")]
        rinv_ready = [sem("rinv_ready0"), sem("rinv_ready1")]
        probs_ready = [sem("probs_ready0"), sem("probs_ready1")]
        pt_filled = [sem("pt_filled0"), sem("pt_filled1")]
        pt_copied = [sem("pt_copied0"), sem("pt_copied1")]
        ot_filled, ot_hi_ready, ot_copied = sem("ot_filled"), sem("ot_hi_ready"), sem("ot_copied")
        y_filled, y_ready = sem("y_filled"), sem("y_ready")
        stats_ready, var_ready = sem("stats_ready"), sem("var_ready")
        eps_added, rstd_ready = sem("eps_added"), sem("rstd_ready")
        centred_ready, out_ready = sem("centred_ready"), sem("out_ready")
        out_stored = [sem(f"out_stored{s}") for s in range(G)]

        x_g = x.rearrange("(t g) n d -> t n g d", g=G)
        xT_g = xT.rearrange("(t g) (c p) n -> t p g c n", g=G, p=P)
        adj_g = adj.rearrange("(t g) n m -> t n g m", g=G)
        out_g = out.rearrange("(t g) n d -> t g n d", g=G)

        def at_least(eng, semaphore, value):
            if not (isinstance(value, int) and value <= 0):
                eng.wait_ge(semaphore, value)

        def wait_apart(eng, semaphore, value):
            if not isinstance(value, int):
                value = eng.snap(value)
            eng.wait_ge(weights_loaded, 16 * len(WEIGHTS))
            eng.wait_ge(semaphore, value)

        def use(name, k):
            b, place, lead = WHERE[name]
            t = k - lead
            ahead = [other + (1 if p < place else 0) for p, (_, other) in enumerate(BANK_USES[b])]
            if isinstance(t, int):
                return sum(min(max(t + a, 0), T) for a in ahead)
            return len(ahead) * t + sum(ahead)

        def filled(eng, name, k):
            eng.wait_ge(f_filled[WHERE[name][0]], use(name, k) + 1)

        def drained(eng, name, k):
            eng.wait_ge(f_drained[WHERE[name][0]], use(name, k) + 1)

        def there(k):
            return not isinstance(k, int) or 0 <= k < T

        def over_groups(eng, iteration):
            iteration(-1)
            iteration(0)
            with eng.Fori(1, T - 1) as t:
                iteration(t)
            iteration(T - 1)
            iteration(T)

        WEIGHTS = [
            (fcw_nat[:, :, :], fc_w.rearrange("(c p) n -> p c n", p=P)),
            (fcw[:, :, 0:D], fc_wT.rearrange("(c p) n -> p c n", p=P)),
            (w_in[0][:, :, :], WqT.rearrange("(c p) n -> p c n", p=P)),
            (w_in[1][:, :, :], WkT.rearrange("(c p) n -> p c n", p=P)),
            (w_in[2][:, :, :], WvT.rearrange("(c p) n -> p c n", p=P)),
            (w_in[3][:, :, :], WoT.rearrange("(c p) n -> p c n", p=P)),
            (qk_w[:, :, 0], q_w.rearrange("a (c p) -> p (a c)", p=P)),
            (qk_w[:, :, 1], k_w.rearrange("a (c p) -> p (a c)", p=P)),
            (fcb_col[:, :], fc_b.rearrange("(c p) -> p c", p=P)),
            (bq_col[:, :], bq.rearrange("(c p) -> p c", p=P)),
            (bk_col[:, :], bk.rearrange("(c p) -> p c", p=P)),
            (bv_col[:, :], bv.rearrange("(c p) -> p c", p=P)),
            (fcb[:, :], fc_b.partition_broadcast(P)),
            (bo_row[:, :], bo.partition_broadcast(P)),
            (gamma_row[:, :], gamma.partition_broadcast(P)),
            (beta_row[:, :], beta.partition_broadcast(P)),
            (qkb[:, 0:1], q_b.partition_broadcast(P)),
            (qkb[:, 1:2], k_b.partition_broadcast(P)),
        ]

        block = ctx.enter_context(nc.Block())

        @block.sync
        def _(sp):
            for dst, src in WEIGHTS:
                sp.dma_start(dst, src, allow_slow_non_contiguous=True).then_inc(weights_loaded, 16)

            def load_xT(u):
                if not (isinstance(u, int) and u == 0):
                    filled(sp, LAST_FP, u - 1)
                sp.dma_start(xT_in[:, :, :, :], xT_g[u]).then_inc(xT_loaded, 16)

            def load_x(u):
                at_least(sp, x_b_ready, u)
                sp.dma_start(x_in[:, :, :], x_g[u]).then_inc(x_loaded, 16)

            def load_adj(u):
                at_least(sp, mask_ready, u)
                at_least(sp, clip_ready, u)
                sp.dma_start(adj_in[:, :, :], adj_g[u]).then_inc(adj_loaded, 16)

            def spread_k(u, o):
                drained(sp, f"K{o}", u)
                at_least(sp, s_filled[o], G * u)
                for h in range(HC):
                    q = slice(h * DK, (h + 1) * DK)
                    sp.dma_start(KD[q, o, h, :, :, :].bitcast(F32),
                                 KT[q, o, :, :, :].bitcast(F32)).then_inc(kd_spread[o], 16)

            def store(k, s):
                sp.wait_ge(out_ready, G * k + s + 1)
                sp.dma_start(out_g[k, s], out_sb[:, s, :]).then_inc(out_stored[s], 16)

            def iteration(t):
                if there(t + 2):
                    load_x(t + 2)
                if there(t - 1):
                    store(t - 1, 0)
                if there(t + 2):
                    load_xT(t + 2)
                if there(t - 1):
                    store(t - 1, 1)
                    store(t - 1, 2)
                if there(t + 1):
                    spread_k(t + 1, 0)
                    spread_k(t + 1, 1)
                if there(t - 1):
                    store(t - 1, 3)
                if there(t + 2):
                    load_adj(t + 2)

            load_xT(0)
            load_x(0)
            load_adj(0)
            sp.wait_ge(kd_zeroed, 1)
            iteration(-1)
            iteration(0)
            with sp.Fori(1, T - 2) as t:
                iteration(t)
            iteration(T - 2)
            iteration(T - 1)
            iteration(T)
            for s in range(G):
                sp.wait_ge(out_stored[s], 16 * T)

        @block.tensor
        def _(pe):
            mm, tr = nc.tensor.matmul, nc.tensor.transpose
            pe.wait_ge(weights_loaded, 16 * len(WEIGHTS))
            pe.wait_ge(consts_ready, 1)
            for c in range(C):
                for o in range(C):
                    mm(y_ps[:, 2 * c:2 * c + 2], fcw_nat[:, o, c * P:(c + 1) * P], qk_w[:, o, :],
                       start=(o == 0), stop=(o == C - 1))
            for o in range(C):
                last = mm(y_ps[:, 4:6], fcb_col[:, o:o + 1].to_broadcast([P, P]), qk_w[:, o, :],
                          start=(o == 0), stop=(o == C - 1))
            last.then_inc(fold_filled, 1)
            pe.wait_ge(fold_copied, 2)
            for c in range(C):
                last = mm(y_ps[:, 0:D], bv_col[:, c:c + 1].to_broadcast([P, P]), w_in[3][:, c, :],
                          start=(c == 0), stop=(c == C - 1))
            last.then_inc(fold_filled, 1)
            pe.wait_ge(fold_copied, 4)
            pe.wait_ge(weights_split, 4)

            def split_mm(psum, lhsT, rhs):
                steps = [(a, b) for lhs, r in zip(lhsT, rhs) for a, b in ((lhs[0], r[0]), (lhs[0], r[1]), (lhs[1], r[0]))]
                for n, (a, b) in enumerate(steps):
                    last = mm(psum, a, b, start=(n == 0), stop=(n == len(steps) - 1))
                return last

            def fill(name, k):
                at_least(pe, f_drained[WHERE[name][0]], use(name, k))
                return f_ps[WHERE[name][0]]

            def has_filled(last, name):
                last.then_inc(f_filled[WHERE[name][0]], 1)

            def project_x(u, g):
                bank = fill(f"fp{g}", u)
                for c in range(C):
                    last = mm(bank[:, 0:D + 2], xT_in[:, g, c, :], fcw[:, c, :], start=(c == 0), stop=(c == C - 1))
                has_filled(last, f"fp{g}")

            def broadcast_k(u):
                bank = fill("kb", u)
                for g in range(G):
                    drained(pe, f"fp{g}", u)
                    last = tr(bank[:, g * N:(g + 1) * N], fp[:, g, D + 1:D + 2].to_broadcast([P, P]), ident[:, :])
                has_filled(last, "kb")

            def transpose_exp0(u):
                bank = fill("ET", u)
                for g in range(G):
                    pe.wait_ge(exp0_ready, G * u + g + 1)
                    last = tr(bank[:, g * N:(g + 1) * N], exp0[:, g, :], ident[:, :])
                has_filled(last, "ET")

            def aggregate(u, half):
                bank = fill(f"AV{half}", u)
                drained(pe, "ET", u)
                for i in range(2):
                    g = 2 * half + i
                    last = mm(bank[:, i * D:(i + 1) * D], exp0T[:, g, :], fp[:, g, 0:D], start=True, stop=True)
                has_filled(last, f"AV{half}")

            def transpose_x1(u, half):
                bank = fill(f"xT{half}", u)
                drained(pe, f"AV{half}", u)
                for i in range(2):
                    for c in range(C):
                        last = tr(bank[:, (i * C + c) * N:(i * C + c + 1) * N],
                                  x1[:, 2 * half + i, c * P:(c + 1) * P], ident[:, :])
                has_filled(last, f"xT{half}")

            def project(u, name, w, o):
                bank = fill(f"{name}{o}", u)
                last = split_mm(bank[:, :], [[x[:, c, o * P:(o + 1) * P] for x in w] for c in range(C)],
                                [[x[:, :, c, :] for x in x1T] for c in range(C)])
                has_filled(last, f"{name}{o}")

            def values(k, half):
                bank = fill(f"V{half}", k)
                for i in range(2):
                    last = split_mm(bank[:, i * D:(i + 1) * D],
                                    [[x[:, 2 * half + i, c, :] for x in x1T] for c in range(C)],
                                    [[w[:, c, :] for w in wv] for c in range(C)])
                has_filled(last, f"V{half}")

            def scores(k, s, h2):
                if s == 0:
                    drained(pe, f"Q{h2}", k)
                    pe.wait_ge(kd_spread[h2], 16 * HC * (k + 1))
                at_least(pe, exp_ready[h2], G * k + s)
                split_mm(s_ps[h2][:, :], [[q[:, h2, s, :] for q in QT]],
                         [[KD[:, h2, :, part, s, :] for part in range(2)]]).then_inc(s_filled[h2], 1)

            def transpose_probs(k, s, h2):
                n = G * k + s
                at_least(pe, pt_copied[h2], n)
                pe.wait_ge(probs_ready[h2], n + 1)
                for h in range(HC):
                    last = tr(pt_ps[h2][:, h * N:(h + 1) * N], probs[:, s % 2, h2 * HC + h, :], ident[:, :])
                last.then_inc(pt_filled[h2], 1)

            def attend(k, s):
                n = G * k + s
                at_least(pe, ot_copied, n)
                if s % 2 == 0:
                    drained(pe, f"V{s // 2}", k)
                for h2 in range(C):
                    pe.wait_ge(pt_copied[h2], n + 1)
                    for h in range(HC):
                        f0 = (h2 * HC + h) * DK
                        last = mm(ot_ps[h * DK:(h + 1) * DK, h2 * N:(h2 + 1) * N], V[:, s, f0:f0 + DK],
                                  probsT[:, h2 * HC + h, :], start=True, stop=True)
                last.then_inc(ot_filled, 1)

            def project_out(k, s):
                n = G * k + s
                at_least(pe, y_ready, n)
                pe.wait_ge(ot_copied, n + 1)
                split_mm(y_ps[:, 0:D], [[x[:, c, :] for x in OT] for c in range(C)],
                         [[w[:, c, :] for w in wo] for c in range(C)]).then_inc(y_filled, 1)

            def iteration(t):
                if there(t + 1):
                    pe.wait_ge(xT_loaded, 16 * (t + 2))
                    project_x(t + 1, 2)
                if there(t):
                    scores(t, 0, 0)
                if there(t - 1):
                    transpose_probs(t - 1, 3, 1)
                if there(t):
                    scores(t, 0, 1)
                if there(t + 1):
                    project_x(t + 1, 3)
                    project_x(t + 1, 1)
                if there(t):
                    scores(t, 1, 0)
                if there(t + 1):
                    project_x(t + 1, 0)
                if there(t):
                    scores(t, 1, 1)
                if there(t - 1):
                    transpose_probs(t - 1, 3, 0)
                if there(t + 1):
                    broadcast_k(t + 1)
                if there(t - 1):
                    project_out(t - 1, 2)
                    attend(t - 1, 3)
                if there(t):
                    transpose_probs(t, 0, 0)
                    values(t, 0)
                    scores(t, 2, 0)
                if there(t - 1):
                    project_out(t - 1, 3)
                if there(t):
                    values(t, 1)
                if there(t + 1):
                    transpose_exp0(t + 1)
                if there(t):
                    transpose_probs(t, 0, 1)
                    scores(t, 2, 1)
                if there(t + 1):
                    aggregate(t + 1, 0)
                    aggregate(t + 1, 1)
                if there(t):
                    scores(t, 3, 0)
                if there(t + 1):
                    transpose_x1(t + 1, 0)
                if there(t):
                    attend(t, 0)
                if there(t + 1):
                    transpose_x1(t + 1, 1)
                if there(t):
                    scores(t, 3, 1)
                    transpose_probs(t, 1, 1)
                    project_out(t, 0)
                if there(t + 1):
                    drained(pe, "xT0", t + 1)
                    drained(pe, "xT1", t + 1)
                    project(t + 1, "K", wk, 0)
                if there(t):
                    transpose_probs(t, 1, 0)
                if there(t + 1):
                    project(t + 1, "K", wk, 1)
                if there(t):
                    attend(t, 1)
                    transpose_probs(t, 2, 1)
                    transpose_probs(t, 2, 0)
                if there(t + 1):
                    project(t + 1, "Q", wq, 1)
                    project(t + 1, "Q", wq, 0)
                if there(t):
                    project_out(t, 1)
                    attend(t, 2)

            over_groups(pe, iteration)

        @block.scalar
        def _(act):
            fn = nc.scalar.activation

            def bank_of(name, k):
                filled(act, name, k)
                return f_ps[WHERE[name][0]]

            def has_drained(op, name):
                op.then_inc(f_drained[WHERE[name][0]], 1)

            def copy_fp(u, g):
                bank = bank_of(f"fp{g}", u)
                has_drained(fn(fp[:, g, :], bank[:, 0:D + 2], ACT.Copy), f"fp{g}")

            def exp_first_layer(u):
                act.wait_ge(leaky_ready, u + 1)
                act.wait_ge(neg_leaky_ready, u + 1)
                for g in range(G):
                    fn(exp0[:, g, :], leaky[:, g, :], ACT.Exp, bias=neg_leaky_max[:, g:g + 1],
                       accum_out=sum0[:, g:g + 1]).then_inc(exp0_ready, 1)

            def copy_exp0T(u):
                bank = bank_of("ET", u)
                has_drained(fn(exp0T[:, :, :], bank[:, :], ACT.Copy), "ET")

            def upper_x1T(u, half):
                bank = bank_of(f"xT{half}", u)
                fn(x1T[0][:, 2 * half:2 * half + 2, :, :], bank[:, :], ACT.Copy).then_inc(x1T_hi_ready[half], 1)

            def upper_k(u, o):
                bank = bank_of(f"K{o}", u)
                if not (isinstance(u, int) and u == 0):
                    act.wait_ge(kd_spread[o], 16 * HC * u)
                fn(KT[:, o, 0, :, :], bank[:, :], ACT.Identity, bias=bk_col[:, o:o + 1]).then_inc(k_hi_ready[o], 1)

            def upper_q(u, o):
                bank = bank_of(f"Q{o}", u)
                at_least(act, s_filled[o], G * u)
                fn(QT[0][:, o, :, :], bank[:, :], ACT.Identity,
                   bias=bq_scaled[:, o:o + 1]).then_inc(q_hi_ready[o], 1)

            def copy_v(k, half):
                bank = bank_of(f"V{half}", k)
                has_drained(fn(V[:, 2 * half:2 * half + 2, :], bank[:, :], ACT.Copy), f"V{half}")

            def exp_scores(k, s, h2):
                act.wait_ge(max_ready[h2], G * k + s + 1)
                for h in range(HC):
                    last = fn(probs[:, s % 2, h2 * HC + h, :], s_ps[h2][:, h * N:(h + 1) * N], ACT.Exp,
                              bias=neg_max[:, h2 * HC + h:h2 * HC + h + 1])
                last.then_inc(exp_ready[h2], 1)

            def copy_probsT(k, s, h2):
                act.wait_ge(pt_filled[h2], G * k + s + 1)
                fn(probsT[:, h2 * HC:(h2 + 1) * HC, :], pt_ps[h2][:, :], ACT.Copy).then_inc(pt_copied[h2], 1)

            def upper_ot(k, s):
                act.wait_ge(ot_filled, G * k + s + 1)
                fn(OT[0][:, :, :], ot_ps[:, 0:C * N], ACT.Copy).then_inc(ot_hi_ready, 1)

            def iteration(t):
                if there(t + 1):
                    copy_fp(t + 1, 2)
                if there(t):
                    exp_scores(t, 0, 0)
                if there(t + 1):
                    copy_fp(t + 1, 3)
                if there(t):
                    exp_scores(t, 0, 1)
                if there(t + 1):
                    copy_fp(t + 1, 1)
                    copy_fp(t + 1, 0)
                if there(t - 1):
                    copy_probsT(t - 1, 3, 0)
                if there(t):
                    exp_scores(t, 1, 0)
                if there(t - 1):
                    upper_ot(t - 1, 3)
                if there(t):
                    exp_scores(t, 1, 1)
                    copy_probsT(t, 0, 0)
                    copy_v(t, 0)
                if there(t + 1):
                    exp_first_layer(t + 1)
                    copy_exp0T(t + 1)
                if there(t):
                    copy_v(t, 1)
                    exp_scores(t, 2, 0)
                    exp_scores(t, 2, 1)
                    copy_probsT(t, 0, 1)
                if there(t + 1):
                    upper_x1T(t + 1, 0)
                if there(t):
                    upper_ot(t, 0)
                if there(t + 1):
                    upper_x1T(t + 1, 1)
                if there(t):
                    copy_probsT(t, 1, 1)
                if there(t + 1):
                    upper_k(t + 1, 0)
                if there(t):
                    copy_probsT(t, 1, 0)
                    exp_scores(t, 3, 1)
                if there(t + 1):
                    upper_k(t + 1, 1)
                if there(t):
                    upper_ot(t, 1)
                    exp_scores(t, 3, 0)
                    copy_probsT(t, 2, 0)
                if there(t + 1):
                    upper_q(t + 1, 1)
                if there(t):
                    copy_probsT(t, 2, 1)
                if there(t + 1):
                    upper_q(t + 1, 0)
                if there(t):
                    upper_ot(t, 2)
                    copy_probsT(t, 3, 1)

            act.wait_ge(weights_loaded, 16 * len(WEIGHTS))
            fn(bq_scaled[:, :], bq_col[:, :], ACT.Copy, scale=SCALE).then_inc(weights_hi, 1)
            for n, w in enumerate((wq, wk, wv, wo)):
                fn(w[0][:, :, :], w_in[n][:, :, :], ACT.Copy, scale=SCALE if n == 0 else 1.0).then_inc(weights_hi, 1)
            act.wait_ge(weights_hi, 1)
            over_groups(act, iteration)

        @block.vector
        def _(dve):
            v = nc.vector

            def bank_of(name, k):
                filled(dve, name, k)
                return f_ps[WHERE[name][0]]

            def has_drained(op, name):
                op.then_inc(f_drained[WHERE[name][0]], 1)

            def make_mask(u):
                dve.wait_ge(adj_loaded, 16 * (u + 1))
                v.tensor_scalar(mask[:, :, :], adj_in[:, :, :], 1.0, -NEG, ALU.subtract,
                                ALU.mult).then_inc(mask_ready, 1)

            def clip_adj(u):
                at_least(dve, masked_ready[0], G * u)
                at_least(dve, masked_ready[1], G * u)
                v.tensor_scalar(adj_clip[:, :, :], adj_in[:, :, :], CLIP, None, ALU.max).then_inc(clip_ready, 1)

            def bias_q(u):
                for g in range(G):
                    drained(dve, f"fp{g}", u)
                v.tensor_scalar(q_eff[:, :], fp[:, :, D], logit_bias[:, 0:1], None, ALU.add).then_inc(q_eff_ready, 1)

            def make_logits(u):
                bank = bank_of("kb", u)
                dve.wait_ge(mask_ready, u + 1)
                dve.wait_ge(q_eff_ready, u + 1)
                for g in range(G):
                    last = v.scalar_tensor_tensor(logit[:, g, :], bank[:, g * N:(g + 1) * N],
                                                  q_eff[:, g:g + 1], mask[:, g, :], ALU.add, ALU.add)
                has_drained(last, "kb")

            def max_logits(u):
                drained(dve, "kb", u)
                v.tensor_reduce(neg_max0[:, :], logit[:, :, :], AX_X, ALU.max, negate=True).then_inc(max0_ready, 1)

            def leaky_relu(u):
                v.scalar_tensor_tensor(leaky[:, :, :], logit[:, :, :], SLOPE, logit[:, :, :],
                                       ALU.mult, ALU.max).then_inc(leaky_ready, 1)

            def leaky_max(u):
                dve.wait_ge(max0_ready, u + 1)
                v.scalar_tensor_tensor(neg_leaky_max[:, :], neg_max0[:, :], SLOPE, neg_max0[:, :],
                                       ALU.mult, ALU.min).then_inc(neg_leaky_ready, 1)

            def invert_sum0(u):
                dve.wait_ge(exp0_ready, G * (u + 1))
                v.reciprocal(rinv0[:, :], sum0[:, :]).then_inc(rinv0_ready, 1)

            def make_x1(u, half):
                bank = bank_of(f"AV{half}", u)
                dve.wait_ge(rinv0_ready, u + 1)
                dve.wait_ge(x_b_ready, u + 1)
                at_least(dve, resid_ready, u)
                for i in range(2):
                    g = 2 * half + i
                    last = v.scalar_tensor_tensor(x1[:, g, :], bank[:, i * D:(i + 1) * D],
                                                  rinv0[:, g:g + 1], x_b[:, g, :], ALU.mult, ALU.add)
                has_drained(last, f"AV{half}")

            def lower_x1T(u, half):
                bank = f_ps[WHERE[f"xT{half}"][0]]
                dve.wait_ge(x1T_hi_ready[half], u + 1)
                gs = slice(2 * half, 2 * half + 2)
                has_drained(v.tensor_tensor(x1T[1][:, gs, :, :],
                                            bank[:, :].rearrange("p (g c n) -> p g c n", g=2, c=C),
                                            x1T[0][:, gs, :, :].bitcast(F32), ALU.subtract), f"xT{half}")

            def lower_k(u, o):
                bank = f_ps[WHERE[f"K{o}"][0]]
                dve.wait_ge(k_hi_ready[o], u + 1)
                has_drained(v.scalar_tensor_tensor(KT[:, o, 1, :, :], bank[:, :].rearrange("p (g n) -> p g n", g=G),
                                                   bk_col[:, o:o + 1], KT[:, o, 0, :, :].bitcast(F32),
                                                   ALU.add, ALU.subtract), f"K{o}")

            def lower_q(u, o):
                bank = f_ps[WHERE[f"Q{o}"][0]]
                dve.wait_ge(q_hi_ready[o], u + 1)
                has_drained(v.scalar_tensor_tensor(QT[1][:, o, :, :], bank[:, :].rearrange("p (g n) -> p g n", g=G),
                                                   bq_scaled[:, o:o + 1], QT[0][:, o, :, :].bitcast(F32),
                                                   ALU.add, ALU.subtract), f"Q{o}")

            def row_max(k, s, h2):
                dve.wait_ge(s_filled[h2], G * k + s + 1)
                v.tensor_reduce(neg_max[:, h2 * HC:(h2 + 1) * HC],
                                s_ps[h2][:, :].rearrange("p (h n) -> p h n", h=HC), AX_X, ALU.max,
                                negate=True).then_inc(max_ready[h2], 1)

            def row_sum(k, s, h2):
                n = G * k + s
                hs = slice(h2 * HC, (h2 + 1) * HC)
                dve.wait_ge(masked_ready[h2], n + 1)
                v.tensor_reduce(sums[:, s % 2, hs], probs[:, s % 2, hs, :], AX_X, ALU.add).then_inc(sum_ready[h2], 1)
                dve.wait_ge(sum_ready[h2], n + 1)
                v.reciprocal(rinv[:, s % 2, hs], sums[:, s % 2, hs]).then_inc(rinv_ready[h2], 1)

            def lower_ot(k, s):
                dve.wait_ge(ot_hi_ready, G * k + s + 1)
                v.tensor_tensor(OT[1][:, :, :], ot_ps[:, 0:C * N].rearrange("p (c n) -> p c n", c=C),
                                OT[0][:, :, :].bitcast(F32), ALU.subtract).then_inc(ot_copied, 1)

            def add_residual(k, s):
                n = G * k + s
                dve.wait_ge(y_filled, n + 1)
                if s == 0:
                    dve.wait_ge(resid_ready, k + 1)
                at_least(dve, rstd_ready, n - 1)
                v.tensor_tensor(y[:, s % 2, :], y_ps[:, 0:D], resid[:, s, :], ALU.add).then_inc(y_ready, 1)
                dve.wait_ge(y_ready, n + 1)
                v.bn_stats(stats[:, :], y[:, s % 2, :]).then_inc(stats_ready, 1)

            def mean_variance(k, s):
                n = G * k + s
                wait_apart(dve, stats_ready, n + 1)
                v.bn_aggr(mean_var[:, s % 2, :], stats[:, :]).then_inc(var_ready, 1)

            def centre(k, s):
                dve.wait_ge(var_ready, G * k + s + 1)
                at_least(dve, out_ready, G * k + s - 1)
                v.scalar_tensor_tensor(centred[:, s % 2, :], y[:, s % 2, :], mean_var[:, s % 2, 0:1], gamma_row[:, :],
                                       ALU.subtract, ALU.mult).then_inc(centred_ready, 1)

            def scale_rows(k, s):
                n = G * k + s
                dve.wait_ge(centred_ready, n + 1)
                dve.wait_ge(rstd_ready, n + 1)
                at_least(dve, out_stored[s], 16 * k)
                v.scalar_tensor_tensor(out_sb[:, s, :], centred[:, s % 2, :], rstd[:, s % 2, 0:1], beta_row[:, :],
                                       ALU.mult, ALU.add).then_inc(out_ready, 1)

            def iteration(t):
                if there(t - 1):
                    row_sum(t - 1, 3, 0)
                if there(t):
                    row_max(t, 0, 0)
                if there(t - 1):
                    add_residual(t - 1, 1)
                if there(t):
                    row_max(t, 0, 1)
                if there(t - 1):
                    mean_variance(t - 1, 1)
                    scale_rows(t - 1, 0)
                if there(t + 1):
                    make_mask(t + 1)
                if there(t - 1):
                    centre(t - 1, 1)
                    lower_ot(t - 1, 2)
                if there(t):
                    row_sum(t, 0, 0)
                    row_max(t, 1, 0)
                if there(t + 1):
                    bias_q(t + 1)
                if there(t):
                    row_max(t, 1, 1)
                if there(t + 1):
                    make_logits(t + 1)
                if there(t - 1):
                    add_residual(t - 1, 2)
                if there(t + 1):
                    max_logits(t + 1)
                if there(t - 1):
                    lower_ot(t - 1, 3)
                if there(t + 1):
                    leaky_max(t + 1)
                    leaky_relu(t + 1)
                if there(t):
                    row_sum(t, 0, 1)
                if there(t - 1):
                    mean_variance(t - 1, 2)
                    add_residual(t - 1, 3)
                if there(t):
                    row_max(t, 2, 0)
                if there(t - 1):
                    scale_rows(t - 1, 1)
                if there(t + 1):
                    invert_sum0(t + 1)
                if there(t):
                    row_sum(t, 1, 1)
                    row_max(t, 2, 1)
                if there(t - 1):
                    mean_variance(t - 1, 3)
                    centre(t - 1, 2)
                if there(t + 1):
                    make_x1(t + 1, 0)
                    make_x1(t + 1, 1)
                if there(t):
                    row_sum(t, 1, 0)
                if there(t + 1):
                    lower_x1T(t + 1, 0)
                if there(t):
                    lower_ot(t, 0)
                if there(t + 1):
                    lower_x1T(t + 1, 1)
                if there(t - 1):
                    scale_rows(t - 1, 2)
                if there(t):
                    row_sum(t, 2, 1)
                    row_max(t, 3, 1)
                    row_sum(t, 2, 0)
                if there(t + 1):
                    lower_k(t + 1, 0)
                if there(t):
                    row_max(t, 3, 0)
                    add_residual(t, 0)
                    lower_ot(t, 1)
                    mean_variance(t, 0)
                if there(t + 1):
                    lower_k(t + 1, 1)
                if there(t - 1):
                    centre(t - 1, 3)
                if there(t):
                    row_sum(t, 3, 1)
                if there(t - 1):
                    scale_rows(t - 1, 3)
                if there(t + 1):
                    lower_q(t + 1, 1)
                    clip_adj(t + 1)
                    lower_q(t + 1, 0)
                if there(t):
                    centre(t, 0)

            v.memset(KD[:, :, :, :, :, :].bitcast(F32), 0.0).then_inc(kd_zeroed, 1)
            dve.wait_ge(weights_loaded, 16 * len(WEIGHTS))
            dve.wait_ge(fold_filled, 1)
            v.tensor_copy(fcw[:, :, D:D + 2],
                          y_ps[:, 0:4].rearrange("p (c w) -> p c w", c=C)).then_inc(fold_copied, 1)
            v.tensor_tensor(qkb[:, :], y_ps[:, 4:6], qkb[:, :], ALU.add).then_inc(fold_copied, 1)
            dve.wait_ge(fold_copied, 2)
            v.tensor_tensor(logit_bias[:, :], qkb[:, 0:1], qkb[:, 1:2], ALU.add).then_inc(fold_copied, 1)
            dve.wait_ge(fold_filled, 2)
            v.tensor_tensor(bo_row[:, :], y_ps[:, 0:D], bo_row[:, :], ALU.add).then_inc(fold_copied, 1)
            dve.wait_ge(fold_copied, 4)
            dve.wait_ge(weights_hi, 5)
            for n, w in enumerate((wq, wk, wv, wo)):
                v.scalar_tensor_tensor(w[1][:, :, :], w_in[n][:, :, :], SCALE if n == 0 else 1.0,
                                       w[0][:, :, :].bitcast(F32), ALU.mult, ALU.subtract).then_inc(weights_split, 1)
            over_groups(dve, iteration)

        @block.gpsimd
        def _(pool):
            g_ = nc.gpsimd

            def add_fc_bias(u):
                if not (isinstance(u, int) and u == 0):
                    drained(pool, LAST_AV, u - 1)
                pool.wait_ge(x_loaded, 16 * (u + 1))
                g_.tensor_tensor(x_b[:, :, :], x_in[:, :, :], fcb[:, :].unsqueeze(1).to_broadcast([P, G, D]),
                                 ALU.add).then_inc(x_b_ready, 1)
            def add_out_bias(k):
                drained(pool, LAST_AV, k)
                at_least(pool, y_ready, G * k)
                g_.tensor_tensor(resid[:, :, :], x1[:, :, :], bo_row[:, :].unsqueeze(1).to_broadcast([P, G, D]),
                                 ALU.add).then_inc(resid_ready, 1)

            def mask_probs(k, s, h2):
                hs = slice(h2 * HC, (h2 + 1) * HC)
                if s == 0:
                    pool.wait_ge(clip_ready, k + 1)
                pool.wait_ge(exp_ready[h2], G * k + s + 1)
                g_.tensor_tensor(probs[:, s % 2, hs, :], probs[:, s % 2, hs, :],
                                 adj_clip[:, s:s + 1, :].to_broadcast([P, HC, N]), ALU.mult).then_inc(masked_ready[h2], 1)

            def scale_probs(k, s, h2):
                hs = slice(h2 * HC, (h2 + 1) * HC)
                pool.wait_ge(rinv_ready[h2], G * k + s + 1)
                g_.tensor_tensor(probs[:, s % 2, hs, :], probs[:, s % 2, hs, :],
                                 rinv[:, s % 2, hs].unsqueeze(2).to_broadcast([P, HC, N]),
                                 ALU.mult).then_inc(probs_ready[h2], 1)

            def inverse_deviation(k, s):
                n = G * k + s
                pool.wait_ge(var_ready, n + 1)
                g_.tensor_tensor(var_eps[:, s % 2, :], mean_var[:, s % 2, 1:2], eps_col[:, :], ALU.add).then_inc(eps_added, 1)
                pool.wait_ge(eps_added, n + 1)
                at_least(pool, out_ready, n - 1)
                g_.tensor_tensor(rstd[:, s % 2, :], var_eps[:, s % 2, :], halves[:, :], ALU.pow).then_inc(rstd_ready, 1)

            def iteration(t):
                if there(t + 1):
                    add_fc_bias(t + 1)
                if there(t - 1):
                    scale_probs(t - 1, 3, 0)
                if there(t):
                    mask_probs(t, 0, 0)
                    scale_probs(t, 0, 0)
                    mask_probs(t, 0, 1)
                if there(t - 1):
                    inverse_deviation(t - 1, 1)
                if there(t):
                    mask_probs(t, 1, 0)
                    mask_probs(t, 1, 1)
                    scale_probs(t, 0, 1)
                    add_out_bias(t)
                    scale_probs(t, 1, 1)
                    mask_probs(t, 2, 1)
                if there(t - 1):
                    inverse_deviation(t - 1, 2)
                if there(t):
                    scale_probs(t, 1, 0)
                    mask_probs(t, 2, 0)
                    scale_probs(t, 2, 1)
                if there(t - 1):
                    inverse_deviation(t - 1, 3)
                if there(t):
                    scale_probs(t, 2, 0)
                    mask_probs(t, 3, 1)
                    mask_probs(t, 3, 0)
                    scale_probs(t, 3, 1)
                    inverse_deviation(t, 0)

            g_.memset(ident[:, :], 0.0).then_inc(ident_step, 1)
            g_.memset(halves[:, :], -0.5).then_inc(ident_step, 1)
            g_.memset(eps_col[:, :], EPS).then_inc(ident_step, 1)
            pool.wait_ge(ident_step, 3)
            g_.affine_select(out=ident[:, :], in_=ident[:, :], compare_op=ALU.not_equal, fill=1.0, base=0,
                             pattern=[[-1, P]], channel_multiplier=1).then_inc(consts_ready, 1)
            pool.wait_ge(consts_ready, 1)
            pool.wait_ge(fold_copied, 4)
            over_groups(pool, iteration)


_INS = ["x", "xT", "adj", "fc_w", "fc_wT", "fc_b", "q_w", "q_b", "k_w", "k_b",
        "WqT", "bq", "WkT", "bk", "WvT", "bv", "WoT", "bo", "gamma", "beta"]


def kernel(x, adj, L0_gnn_fc_w, L0_gnn_fc_b, L0_gnn_q_w, L0_gnn_q_b, L0_gnn_k_w, L0_gnn_k_b,
           L1_gnn_Wq, L1_gnn_bq, L1_gnn_Wk, L1_gnn_bk, L1_gnn_Wv, L1_gnn_bv, L1_gnn_Wo, L1_gnn_bo,
           L1_gnn_gamma, L1_gnn_beta):
    import numpy as np
    import concourse.bacc as bacc
    from concourse.bass_utils import run_bass_kernel_spmd

    given = dict(
        x=x, xT=np.transpose(np.asarray(x), (0, 2, 1)), adj=adj,
        fc_w=L0_gnn_fc_w, fc_wT=np.asarray(L0_gnn_fc_w).T, fc_b=L0_gnn_fc_b,
        q_w=L0_gnn_q_w, q_b=L0_gnn_q_b, k_w=L0_gnn_k_w, k_b=L0_gnn_k_b,
        WqT=np.asarray(L1_gnn_Wq).T, bq=L1_gnn_bq, WkT=np.asarray(L1_gnn_Wk).T, bk=L1_gnn_bk,
        WvT=np.asarray(L1_gnn_Wv).T, bv=L1_gnn_bv, WoT=np.asarray(L1_gnn_Wo).T, bo=L1_gnn_bo,
        gamma=L1_gnn_gamma, beta=L1_gnn_beta,
    )
    nc = bacc.Bacc("TRN2", target_bir_lowering=False, num_devices=1)
    arrays, args = {}, []
    for name in _INS:
        a = np.ascontiguousarray(given[name])
        arrays[f"in_{name}"] = a
        args.append(nc.dram_tensor(f"in_{name}", a.shape, mybir.dt.from_np(a.dtype), kind="ExternalInput").ap())
    out = nc.dram_tensor("out", (B, N, D), F32, kind="ExternalOutput").ap()
    gat_then_attention(nc, *args, out)
    r = run_bass_kernel_spmd(nc, [arrays], core_ids=[0])
    return r.results[0]["out"]
```

```python
from contextlib import ExitStack

import concourse.bass as bass
from concourse import mybir

B, N, D = 128, 128, 256
H = 8
DK = D // H
P = 128
C = D // P
HC = H // C
G = 4
T = B // G
NEG = -1.0e9
SLOPE = 0.01
CLIP = 1e-8
EPS = 1e-5
SCALE = float(DK) ** -0.5

F32 = mybir.dt.float32
F32R = mybir.dt.float32r
ALU = mybir.AluOpType
ACT = mybir.ActivationFunctionType
AX_X = mybir.AxisListType.X

BANK_USES = [
    [("fp1", 1), ("fp0", 1), ("V0", 0), ("ET", 1), ("AV0", 1), ("xT0", 1), ("Q1", 1), ("Q0", 1)],
    [("fp2", 1), ("fp3", 1), ("kb", 1), ("V1", 0), ("AV1", 1), ("xT1", 1), ("K1", 1), ("K0", 1)],
]
WHERE = {name: (b, place, lead) for b, uses in enumerate(BANK_USES) for place, (name, lead) in enumerate(uses)}
FPS = [f"fp{g}" for g in range(G)]
LAST_FP, LAST_AV = "fp0", "AV1"


def gat_then_attention(nc, x, xT, adj, fc_w, fc_wT, vectors, qk_b, wT, row_vectors, out):
    with ExitStack() as ctx:
        def sb(name, *shape):
            return ctx.enter_context(nc.sbuf_tensor(name, [P, *shape], F32))

        def halves_of(name, *shape):
            return tuple(ctx.enter_context(nc.sbuf_tensor(f"{name}_{part}", [P, *shape], F32R))
                         for part in ("hi", "lo"))

        def bank(name):
            return ctx.enter_context(nc.psum_tensor(name, [P, 512], F32))

        def sem(name):
            return ctx.enter_context(nc.semaphore(name))

        ident = sb("ident", P)
        halves = sb("halves", 1)
        eps_col, minus_one = sb("eps_col", 1), sb("minus_one", 1)
        fcw_nat = sb("fcw_nat", C, D)
        fcw_in = sb("fcw_in", C, D + 2)
        fcw = halves_of("fcw", C, D + 2)
        cols = sb("cols", C, 6)
        qk_w, fcb_col, bq_col, bk_col, bv_col = (cols[:, :, a:b] for a, b in ((0, 2), (2, 3), (3, 4), (4, 5), (5, 6)))
        qkb = sb("qkb", 2)
        logit_bias = sb("logit_bias", 1)
        w_in = sb("w_in", 4, C, D)
        wq, wk, wv, wo = (halves_of(n, C, D) for n in ("wq", "wk", "wv", "wo"))
        bq_scaled = sb("bq_scaled", C)
        rows = sb("rows", 4, D)
        fcb, bo_row, gamma_row, beta_row = (rows[:, i, :] for i in range(4))
        x_in = sb("x_in", G, D)
        x_b = sb("x_b", G, D)
        xT_in = sb("xT_in", G, C, N)
        xT_parts = halves_of("xT", G, C, N)
        adj_in = sb("adj_in", G, N)
        mask = sb("mask", G, N)
        fp = sb("fp", G, D + 2)
        q_eff = sb("q_eff", G)
        logit = sb("logit", G, N)
        leaky = sb("leaky", G, N)
        neg_max0 = sb("neg_max0", G)
        neg_leaky_max = sb("neg_leaky_max", G)
        exp0 = sb("exp0", G, N)
        sum0 = sb("sum0", G)
        rinv0 = sb("rinv0", G)
        exp0T = sb("exp0T", G, N)
        x1 = sb("x1", G, D)
        x1T = halves_of("x1T", G, C, N)
        resid = sb("resid", G, D)
        adj_clip = sb("adj_clip", G, N)
        QT = halves_of("QT", C, G, N)
        KT = ctx.enter_context(nc.sbuf_tensor("KT", [P, C, 2, G, N], F32R))
        KD = ctx.enter_context(nc.sbuf_tensor("KD", [P, C, HC, 2, G, N], F32R))
        V = sb("V", G, D)
        neg_max = sb("neg_max", H)
        probs = sb("probs", 2, H, N)
        sums = sb("sums", 2, H)
        rinv = sb("rinv", 2, H)
        probsT = sb("probsT", H, N)
        OT = halves_of("OT", C, N)
        y = sb("y", 2, D)
        stats = sb("stats", 2, 6)
        mean_var = sb("mean_var", 2, 2)
        var_eps = sb("var_eps", 2, 1)
        rstd = sb("rstd", 2, 1)
        neg_mean = sb("neg_mean", 2, 1)
        shift = sb("shift", 2, 1)
        scaled = sb("scaled", 2, D)
        out_gamma = sb("out_gamma", 2, D)
        out_sb = sb("out_sb", G, D)

        s_ps = [bank("s_ps0"), bank("s_ps1")]
        pt_ps = [bank("pt_ps0"), bank("pt_ps1")]
        f_ps = [bank("f_ps0"), bank("f_ps1")]
        ot_ps = bank("ot_ps")
        y_ps = bank("y_ps")

        folded_loaded, weights_loaded = sem("folded_loaded"), sem("weights_loaded")
        ident_step = sem("ident_step")
        consts_ready = sem("consts_ready")
        kd_zeroed = sem("kd_zeroed")
        fold_filled = sem("fold_filled")
        fold_copied = sem("fold_copied")
        fcw_hi_ready = sem("fcw_hi_ready")
        weights_hi, weights_split = sem("weights_hi"), sem("weights_split")
        x_loaded, xT_loaded, adj_loaded = sem("x_loaded"), sem("xT_loaded"), sem("adj_loaded")
        filled = {name: sem(f"filled_{name}") for name in WHERE}
        drained = {name: sem(f"drained_{name}") for name in WHERE}
        xT_hi_ready, xT_split = sem("xT_hi_ready"), sem("xT_split")
        mask_ready = sem("mask_ready")
        leaky_ready = sem("leaky_ready")
        max0_ready = sem("max0_ready")
        neg_leaky_ready = sem("neg_leaky_ready")
        exp0_ready = sem("exp0_ready")
        rinv0_ready = sem("rinv0_ready")
        resid_ready = sem("resid_ready")
        clip_ready = sem("clip_ready")
        x_b_ready = sem("x_b_ready")
        q_eff_ready = sem("q_eff_ready")
        x1T_hi_ready = [sem("x1T_hi_ready0"), sem("x1T_hi_ready1")]
        k_hi_ready = [sem("k_hi_ready0"), sem("k_hi_ready1")]
        q_hi_ready = [sem("q_hi_ready0"), sem("q_hi_ready1")]
        kd_spread = [sem("kd_spread0"), sem("kd_spread1")]
        s_filled = [sem("s_filled0"), sem("s_filled1")]
        max_ready = [sem("max_ready0"), sem("max_ready1")]
        exp_ready = [sem("exp_ready0"), sem("exp_ready1")]
        sum_ready = [sem("sum_ready0"), sem("sum_ready1")]
        rinv_ready = [sem("rinv_ready0"), sem("rinv_ready1")]
        probs_ready = [sem("probs_ready0"), sem("probs_ready1")]
        pt_filled = [sem("pt_filled0"), sem("pt_filled1")]
        pt_copied = [sem("pt_copied0"), sem("pt_copied1")]
        ot_filled, ot_hi_ready, ot_copied = sem("ot_filled"), sem("ot_hi_ready"), sem("ot_copied")
        y_filled, y_ready = sem("y_filled"), sem("y_ready")
        stats_ready, var_ready = sem("stats_ready"), sem("var_ready")
        eps_added, rstd_ready = sem("eps_added"), sem("rstd_ready")
        shift_ready, scaled_ready = sem("shift_ready"), sem("scaled_ready")
        gamma_ready, out_ready = sem("gamma_ready"), sem("out_ready")
        out_stored = [sem(f"out_stored{s}") for s in range(G)]

        x_g = x.rearrange("(t g) n d -> t n g d", g=G)
        xT_g = xT.rearrange("(t g) (c p) n -> t p g c n", g=G, p=P)
        adj_g = adj.rearrange("(t g) n m -> t n g m", g=G)
        out_g = out.rearrange("(t g) n d -> t g n d", g=G)

        def at_least(eng, semaphore, value):
            if not (isinstance(value, int) and value <= 0):
                eng.wait_ge(semaphore, value)

        def wait_apart(eng, semaphore, value):
            if not isinstance(value, int):
                value = eng.snap(value)
            eng.wait_ge(weights_loaded, 16 * len(WEIGHTS))
            eng.wait_ge(semaphore, value)

        def before(name, k):
            b, place, lead = WHERE[name]
            t = k - lead
            while not isinstance(t, int) or t >= -1:
                place -= 1
                if place < 0:
                    place, t = len(BANK_USES[b]) - 1, t - 1
                other, other_lead = BANK_USES[b][place]
                if there(t + other_lead):
                    return other, t + other_lead
            return None, None

        def there(k):
            return not isinstance(k, int) or 0 <= k < T

        def later(k):
            return not isinstance(k, int) or 1 <= k < T

        def over_groups(eng, iteration):
            iteration(-1)
            iteration(0)
            iteration(1)
            with eng.Fori(2, T - 1) as t:
                iteration(t)
            iteration(T - 1)
            iteration(T)

        FOLDED = [
            (fcw_nat[:, :, :], fc_w.rearrange("(c p) n -> p c n", p=P)),
            (cols[:, :, :], vectors),
            (fcw_in[:, :, 0:D], fc_wT.rearrange("(c p) n -> p c n", p=P)),
            (qkb[:, :], qk_b.partition_broadcast(P)),
        ]
        WEIGHTS = [
            (w_in[:, :, :, :], wT.rearrange("w (c p) n -> p w c n", p=P)),
            (rows[:, :, :], row_vectors.partition_broadcast(P)),
        ]

        block = ctx.enter_context(nc.Block())

        @block.sync
        def _(sp):
            for dst, src in FOLDED:
                sp.dma_start(dst, src, allow_slow_non_contiguous=True).then_inc(folded_loaded, 16)

            def load_xT(u):
                at_least(sp, xT_split, u)
                sp.dma_start(xT_in[:, :, :, :], xT_g[u]).then_inc(xT_loaded, 16)

            def load_x(u):
                at_least(sp, x_b_ready, u)
                sp.dma_start(x_in[:, :, :], x_g[u]).then_inc(x_loaded, 16)

            def load_adj(u):
                at_least(sp, mask_ready, u)
                at_least(sp, clip_ready, u)
                sp.dma_start(adj_in[:, :, :], adj_g[u]).then_inc(adj_loaded, 16)

            def spread_k(u, o):
                sp.wait_ge(drained[f"K{o}"], u + 1)
                for h in range(HC):
                    q = slice(h * DK, (h + 1) * DK)
                    sp.dma_start(KD[q, o, h, :, :, :].bitcast(F32),
                                 KT[q, o, :, :, :].bitcast(F32)).then_inc(kd_spread[o], 16)

            def store(k, s):
                sp.wait_ge(out_ready, G * k + s + 1)
                sp.dma_start(out_g[k, s], out_sb[:, s, :]).then_inc(out_stored[s], 16)

            def iteration(t):
                if later(t + 2):
                    load_xT(t + 2)
                    load_x(t + 2)
                if there(t - 1):
                    store(t - 1, 0)
                    store(t - 1, 1)
                    store(t - 1, 2)
                if there(t + 1):
                    spread_k(t + 1, 1)
                if there(t - 1):
                    store(t - 1, 3)
                if there(t + 1):
                    spread_k(t + 1, 0)
                if later(t + 2):
                    load_adj(t + 2)

            load_xT(0)
            for dst, src in WEIGHTS:
                sp.dma_start(dst, src).then_inc(weights_loaded, 16)
            load_adj(0)
            load_x(0)
            sp.wait_ge(kd_zeroed, 1)
            iteration(-1)
            iteration(0)
            iteration(1)
            with sp.Fori(2, T - 2) as t:
                iteration(t)
            iteration(T - 2)
            iteration(T - 1)
            iteration(T)
            for s in range(G):
                sp.wait_ge(out_stored[s], 16 * T)

        @block.tensor
        def _(pe):
            mm, tr = nc.tensor.matmul, nc.tensor.transpose
            pe.wait_ge(folded_loaded, 16 * len(FOLDED))
            pe.wait_ge(consts_ready, 1)
            for c in range(C):
                for o in range(C):
                    mm(y_ps[:, 2 * c:2 * c + 2], fcw_nat[:, o, c * P:(c + 1) * P], qk_w[:, o, :],
                       start=(o == 0), stop=(o == C - 1))
            for o in range(C):
                last = mm(y_ps[:, 4:6], fcb_col[:, o, :].to_broadcast([P, P]), qk_w[:, o, :],
                          start=(o == 0), stop=(o == C - 1))
            last.then_inc(fold_filled, 1)
            pe.wait_ge(fold_copied, 2)
            pe.wait_ge(weights_loaded, 16 * len(WEIGHTS))
            for c in range(C):
                last = mm(y_ps[:, 0:D], bv_col[:, c, :].to_broadcast([P, P]), w_in[:, 3, c, :],
                          start=(c == 0), stop=(c == C - 1))
            last.then_inc(fold_filled, 1)
            pe.wait_ge(weights_split, 1)

            def split_mm(psum, lhsT, rhs):
                steps = [pair for left, right in zip(lhsT, rhs)
                         for pair in ((left[0], right[0]), (left[0], right[1]), (left[1], right[0]))]
                for n, (a, b) in enumerate(steps):
                    last = mm(psum, a, b, start=(n == 0), stop=(n == len(steps) - 1))
                return last

            def fill(name, k):
                other, group = before(name, k)
                if other:
                    pe.wait_ge(drained[other], group + 1)
                return f_ps[WHERE[name][0]]

            def has_filled(last, name):
                last.then_inc(filled[name], 1)

            def project_x(u, g):
                bank = fill(f"fp{g}", u)
                last = split_mm(bank[:, 0:D + 2], [[x[:, g, c, :] for x in xT_parts] for c in range(C)],
                                [[w[:, c, :] for w in fcw] for c in range(C)])
                has_filled(last, f"fp{g}")

            def broadcast_k(u):
                bank = fill("kb", u)
                for g in range(G):
                    last = tr(bank[:, g * N:(g + 1) * N], fp[:, g, D + 1:D + 2].to_broadcast([P, P]), ident[:, :])
                has_filled(last, "kb")

            def transpose_exp0(u):
                bank = fill("ET", u)
                for g in range(G):
                    pe.wait_ge(exp0_ready, G * u + g + 1)
                    last = tr(bank[:, g * N:(g + 1) * N], exp0[:, g, :], ident[:, :])
                has_filled(last, "ET")

            def aggregate(u, half):
                bank = fill(f"AV{half}", u)
                for i in range(2):
                    g = 2 * half + i
                    last = mm(bank[:, i * D:(i + 1) * D], exp0T[:, g, :], fp[:, g, 0:D], start=True, stop=True)
                has_filled(last, f"AV{half}")

            def transpose_x1(u, half):
                bank = fill(f"xT{half}", u)
                for i in range(2):
                    for c in range(C):
                        last = tr(bank[:, (i * C + c) * N:(i * C + c + 1) * N],
                                  x1[:, 2 * half + i, c * P:(c + 1) * P], ident[:, :])
                has_filled(last, f"xT{half}")

            def project(u, name, w, o):
                bank = fill(f"{name}{o}", u)
                if isinstance(u, int) and u == 0:
                    pe.wait_ge(weights_split, 5)
                last = split_mm(bank[:, :], [[x[:, c, o * P:(o + 1) * P] for x in w] for c in range(C)],
                                [[x[:, :, c, :] for x in x1T] for c in range(C)])
                has_filled(last, f"{name}{o}")

            def values(k, half):
                bank = fill(f"V{half}", k)
                for i in range(2):
                    last = split_mm(bank[:, i * D:(i + 1) * D],
                                    [[x[:, 2 * half + i, c, :] for x in x1T] for c in range(C)],
                                    [[w[:, c, :] for w in wv] for c in range(C)])
                has_filled(last, f"V{half}")

            def scores(k, s, h2):
                if s == 0:
                    pe.wait_ge(kd_spread[h2], 16 * HC * (k + 1))
                at_least(pe, exp_ready[h2], G * k + s)
                split_mm(s_ps[h2][:, :], [[q[:, h2, s, :] for q in QT]],
                         [[KD[:, h2, :, part, s, :] for part in range(2)]]).then_inc(s_filled[h2], 1)

            def transpose_probs(k, s, h2):
                n = G * k + s
                at_least(pe, pt_copied[h2], n)
                pe.wait_ge(probs_ready[h2], n + 1)
                for h in range(HC):
                    last = tr(pt_ps[h2][:, h * N:(h + 1) * N], probs[:, s % 2, h2 * HC + h, :], ident[:, :])
                last.then_inc(pt_filled[h2], 1)

            def attend(k, s):
                n = G * k + s
                at_least(pe, ot_copied, n)
                for h2 in range(C):
                    pe.wait_ge(pt_copied[h2], n + 1)
                    for h in range(HC):
                        f0 = (h2 * HC + h) * DK
                        last = mm(ot_ps[h * DK:(h + 1) * DK, h2 * N:(h2 + 1) * N], V[:, s, f0:f0 + DK],
                                  probsT[:, h2 * HC + h, :], start=True, stop=True)
                last.then_inc(ot_filled, 1)

            def project_out(k, s):
                n = G * k + s
                at_least(pe, y_ready, n)
                pe.wait_ge(ot_copied, n + 1)
                split_mm(y_ps[:, 0:D], [[x[:, c, :] for x in OT] for c in range(C)],
                         [[w[:, c, :] for w in wo] for c in range(C)]).then_inc(y_filled, 1)

            def iteration(t):
                if there(t - 1):
                    transpose_probs(t - 1, 3, 0)
                if there(t):
                    scores(t, 0, 1)
                if there(t - 1):
                    project_out(t - 1, 1)
                if there(t + 1):
                    pe.wait_ge(xT_split, t + 2)
                    project_x(t + 1, 2)
                if there(t - 1):
                    pe.wait_ge(drained["V1"], t)
                    attend(t - 1, 2)
                if there(t + 1):
                    project_x(t + 1, 1)
                if there(t):
                    pe.wait_ge(drained["Q0"], t + 1)
                    scores(t, 0, 0)
                    scores(t, 1, 1)
                if there(t + 1):
                    project_x(t + 1, 3)
                if there(t - 1):
                    transpose_probs(t - 1, 3, 1)
                if there(t + 1):
                    project_x(t + 1, 0)
                if there(t - 1):
                    project_out(t - 1, 2)
                if there(t):
                    transpose_probs(t, 0, 1)
                if there(t + 1):
                    pe.wait_ge(drained["fp0"], t + 2)
                    broadcast_k(t + 1)
                if there(t - 1):
                    attend(t - 1, 3)
                if there(t):
                    values(t, 0)
                    scores(t, 1, 0)
                if there(t - 1):
                    project_out(t - 1, 3)
                if there(t):
                    scores(t, 2, 1)
                    values(t, 1)
                if there(t + 1):
                    transpose_exp0(t + 1)
                if there(t):
                    transpose_probs(t, 0, 0)
                    scores(t, 2, 0)
                if there(t + 1):
                    aggregate(t + 1, 0)
                    aggregate(t + 1, 1)
                if there(t):
                    pe.wait_ge(drained["V0"], t + 1)
                    attend(t, 0)
                if there(t + 1):
                    transpose_x1(t + 1, 0)
                if there(t):
                    transpose_probs(t, 1, 0)
                if there(t + 1):
                    transpose_x1(t + 1, 1)
                if there(t):
                    scores(t, 3, 0)
                    transpose_probs(t, 1, 1)
                    scores(t, 3, 1)
                if there(t + 1):
                    pe.wait_ge(drained["xT0"], t + 2)
                    project(t + 1, "K", wk, 1)
                    project(t + 1, "Q", wq, 1)
                if there(t):
                    project_out(t, 0)
                if there(t + 1):
                    project(t + 1, "K", wk, 0)
                if there(t):
                    attend(t, 1)
                    transpose_probs(t, 2, 0)
                if there(t + 1):
                    project(t + 1, "Q", wq, 0)
                if there(t):
                    transpose_probs(t, 2, 1)

            over_groups(pe, iteration)

        @block.scalar
        def _(act):
            fn = nc.scalar.activation

            def bank_of(name, k):
                act.wait_ge(filled[name], k + 1)
                return f_ps[WHERE[name][0]]

            def has_drained(op, name):
                op.then_inc(drained[name], 1)

            def upper_xT(u):
                act.wait_ge(xT_loaded, 16 * (u + 1))
                if not (isinstance(u, int) and u == 0):
                    act.wait_ge(filled[LAST_FP], u)
                fn(xT_parts[0][:, :, :, :], xT_in[:, :, :, :], ACT.Copy).then_inc(xT_hi_ready, 1)

            def copy_fp(u, g):
                bank = bank_of(f"fp{g}", u)
                has_drained(fn(fp[:, g, :], bank[:, 0:D + 2], ACT.Copy), f"fp{g}")

            def exp_first_layer(u):
                act.wait_ge(leaky_ready, u + 1)
                act.wait_ge(neg_leaky_ready, u + 1)
                for g in range(G):
                    fn(exp0[:, g, :], leaky[:, g, :], ACT.Exp, bias=neg_leaky_max[:, g:g + 1],
                       accum_out=sum0[:, g:g + 1]).then_inc(exp0_ready, 1)

            def copy_exp0T(u):
                bank = bank_of("ET", u)
                has_drained(fn(exp0T[:, :, :], bank[:, :], ACT.Copy), "ET")

            def upper_x1T(u, half):
                bank = bank_of(f"xT{half}", u)
                fn(x1T[0][:, 2 * half:2 * half + 2, :, :], bank[:, :], ACT.Copy).then_inc(x1T_hi_ready[half], 1)

            def upper_k(u, o):
                bank = bank_of(f"K{o}", u)
                if not (isinstance(u, int) and u == 0):
                    act.wait_ge(kd_spread[o], 16 * HC * u)
                fn(KT[:, o, 0, :, :], bank[:, :], ACT.Identity, bias=bk_col[:, o, :]).then_inc(k_hi_ready[o], 1)

            def upper_q(u, o):
                bank = bank_of(f"Q{o}", u)
                fn(QT[0][:, o, :, :], bank[:, :], ACT.Identity,
                   bias=bq_scaled[:, o:o + 1]).then_inc(q_hi_ready[o], 1)

            def copy_v(k, half):
                bank = bank_of(f"V{half}", k)
                has_drained(fn(V[:, 2 * half:2 * half + 2, :], bank[:, :], ACT.Copy), f"V{half}")

            def exp_scores(k, s, h2):
                act.wait_ge(max_ready[h2], G * k + s + 1)
                at_least(act, pt_filled[h2], G * k + s - 1)
                for h in range(HC):
                    last = fn(probs[:, s % 2, h2 * HC + h, :], s_ps[h2][:, h * N:(h + 1) * N], ACT.Exp,
                              bias=neg_max[:, h2 * HC + h:h2 * HC + h + 1])
                last.then_inc(exp_ready[h2], 1)

            def copy_probsT(k, s, h2):
                act.wait_ge(pt_filled[h2], G * k + s + 1)
                at_least(act, ot_filled, G * k + s)
                fn(probsT[:, h2 * HC:(h2 + 1) * HC, :], pt_ps[h2][:, :], ACT.Copy).then_inc(pt_copied[h2], 1)

            def upper_ot(k, s):
                act.wait_ge(ot_filled, G * k + s + 1)
                at_least(act, y_filled, G * k + s)
                fn(OT[0][:, :, :], ot_ps[:, 0:C * N], ACT.Copy).then_inc(ot_hi_ready, 1)

            def scale_rows(k, s):
                n, i = G * k + s, s % 2
                act.wait_ge(shift_ready, n + 1)
                at_least(act, out_ready, n - 1)
                fn(scaled[:, i, :], y[:, i, :], ACT.Identity, bias=shift[:, i, :],
                   scale=rstd[:, i, :]).then_inc(scaled_ready, 1)

            def iteration(t):
                if there(t):
                    upper_k(t, 0)
                if later(t + 1):
                    upper_xT(t + 1)
                if there(t - 1):
                    copy_probsT(t - 1, 2, 0)
                    upper_ot(t - 1, 1)
                if there(t):
                    upper_q(t, 0)
                if there(t - 1):
                    copy_probsT(t - 1, 2, 1)
                if there(t):
                    exp_scores(t, 0, 1)
                if there(t + 1):
                    copy_fp(t + 1, 2)
                if there(t - 1):
                    copy_probsT(t - 1, 3, 0)
                    scale_rows(t - 1, 0)
                    upper_ot(t - 1, 2)
                if there(t + 1):
                    copy_fp(t + 1, 1)
                if there(t):
                    exp_scores(t, 0, 0)
                if there(t - 1):
                    copy_probsT(t - 1, 3, 1)
                if there(t + 1):
                    copy_fp(t + 1, 3)
                    copy_fp(t + 1, 0)
                if there(t):
                    exp_scores(t, 1, 1)
                if there(t - 1):
                    scale_rows(t - 1, 1)
                if there(t):
                    copy_probsT(t, 0, 1)
                if there(t - 1):
                    upper_ot(t - 1, 3)
                if there(t):
                    copy_v(t, 0)
                if there(t + 1):
                    exp_first_layer(t + 1)
                if there(t):
                    exp_scores(t, 1, 0)
                if there(t + 1):
                    copy_exp0T(t + 1)
                if there(t):
                    copy_v(t, 1)
                    copy_probsT(t, 0, 0)
                if there(t - 1):
                    scale_rows(t - 1, 2)
                if there(t):
                    exp_scores(t, 2, 0)
                    exp_scores(t, 2, 1)
                if there(t + 1):
                    upper_x1T(t + 1, 0)
                    upper_x1T(t + 1, 1)
                if there(t):
                    upper_ot(t, 0)
                    copy_probsT(t, 1, 1)
                    exp_scores(t, 3, 0)
                if there(t + 1):
                    upper_k(t + 1, 1)
                if there(t):
                    copy_probsT(t, 1, 0)
                if there(t - 1):
                    scale_rows(t - 1, 3)
                if there(t + 1):
                    upper_q(t + 1, 1)
                if there(t):
                    exp_scores(t, 3, 1)

            act.wait_ge(fold_copied, 1)
            fn(fcw[0][:, :, :], fcw_in[:, :, :], ACT.Copy).then_inc(fcw_hi_ready, 1)
            upper_xT(0)
            act.wait_ge(weights_loaded, 16 * len(WEIGHTS))
            fn(bq_scaled[:, :], bq_col[:, :, 0], ACT.Copy, scale=SCALE).then_inc(weights_hi, 1)
            for n, w in enumerate((wq, wk, wv, wo)):
                fn(w[0][:, :, :], w_in[:, n, :, :], ACT.Copy, scale=SCALE if n == 0 else 1.0).then_inc(weights_hi, 1)
            act.wait_ge(weights_hi, 1)
            over_groups(act, iteration)

        @block.vector
        def _(dve):
            v = nc.vector

            def bank_of(name, k):
                dve.wait_ge(filled[name], k + 1)
                return f_ps[WHERE[name][0]]

            def has_drained(op, name):
                op.then_inc(drained[name], 1)

            def make_mask(u):
                dve.wait_ge(adj_loaded, 16 * (u + 1))
                v.tensor_scalar(mask[:, :, :], adj_in[:, :, :], 1.0, -NEG, ALU.subtract,
                                ALU.mult).then_inc(mask_ready, 1)

            def clip_adj(u):
                at_least(dve, sum_ready[0], G * u)
                at_least(dve, sum_ready[1], G * u)
                v.tensor_scalar(adj_clip[:, :, :], adj_in[:, :, :], CLIP, None, ALU.max).then_inc(clip_ready, 1)

            def bias_q(u):
                for name in FPS:
                    dve.wait_ge(drained[name], u + 1)
                v.tensor_scalar(q_eff[:, :], fp[:, :, D], logit_bias[:, 0:1], None, ALU.add).then_inc(q_eff_ready, 1)

            def make_logits(u):
                bank = bank_of("kb", u)
                dve.wait_ge(mask_ready, u + 1)
                dve.wait_ge(q_eff_ready, u + 1)
                for g in range(G):
                    last = v.scalar_tensor_tensor(logit[:, g, :], bank[:, g * N:(g + 1) * N],
                                                  q_eff[:, g:g + 1], mask[:, g, :], ALU.add, ALU.add)
                has_drained(last, "kb")

            def max_logits(u):
                dve.wait_ge(drained["kb"], u + 1)
                v.tensor_reduce(neg_max0[:, :], logit[:, :, :], AX_X, ALU.max, negate=True).then_inc(max0_ready, 1)

            def leaky_relu(u):
                dve.wait_ge(drained["kb"], u + 1)
                v.scalar_tensor_tensor(leaky[:, :, :], logit[:, :, :], SLOPE, logit[:, :, :],
                                       ALU.mult, ALU.max).then_inc(leaky_ready, 1)

            def leaky_max(u):
                dve.wait_ge(max0_ready, u + 1)
                v.scalar_tensor_tensor(neg_leaky_max[:, :], neg_max0[:, :], SLOPE, neg_max0[:, :],
                                       ALU.mult, ALU.min).then_inc(neg_leaky_ready, 1)

            def invert_sum0(u):
                dve.wait_ge(exp0_ready, G * (u + 1))
                v.reciprocal(rinv0[:, :], sum0[:, :]).then_inc(rinv0_ready, 1)

            def make_x1(u, half):
                bank = bank_of(f"AV{half}", u)
                dve.wait_ge(rinv0_ready, u + 1)
                dve.wait_ge(x_b_ready, u + 1)
                at_least(dve, resid_ready, u)
                for i in range(2):
                    g = 2 * half + i
                    last = v.scalar_tensor_tensor(x1[:, g, :], bank[:, i * D:(i + 1) * D],
                                                  rinv0[:, g:g + 1], x_b[:, g, :], ALU.mult, ALU.add)
                has_drained(last, f"AV{half}")

            def lower_x1T(u, half):
                bank = f_ps[WHERE[f"xT{half}"][0]]
                dve.wait_ge(x1T_hi_ready[half], u + 1)
                gs = slice(2 * half, 2 * half + 2)
                has_drained(v.tensor_tensor(x1T[1][:, gs, :, :],
                                            bank[:, :].rearrange("p (g c n) -> p g c n", g=2, c=C),
                                            x1T[0][:, gs, :, :].bitcast(F32), ALU.subtract), f"xT{half}")

            def lower_k(u, o):
                bank = f_ps[WHERE[f"K{o}"][0]]
                dve.wait_ge(k_hi_ready[o], u + 1)
                has_drained(v.scalar_tensor_tensor(KT[:, o, 1, :, :], bank[:, :].rearrange("p (g n) -> p g n", g=G),
                                                   bk_col[:, o, :], KT[:, o, 0, :, :].bitcast(F32),
                                                   ALU.add, ALU.subtract), f"K{o}")

            def lower_q(u, o):
                bank = f_ps[WHERE[f"Q{o}"][0]]
                dve.wait_ge(q_hi_ready[o], u + 1)
                has_drained(v.scalar_tensor_tensor(QT[1][:, o, :, :], bank[:, :].rearrange("p (g n) -> p g n", g=G),
                                                   bq_scaled[:, o:o + 1], QT[0][:, o, :, :].bitcast(F32),
                                                   ALU.add, ALU.subtract), f"Q{o}")

            def row_max(k, s, h2):
                dve.wait_ge(s_filled[h2], G * k + s + 1)
                v.tensor_reduce(neg_max[:, h2 * HC:(h2 + 1) * HC],
                                s_ps[h2][:, :].rearrange("p (h n) -> p h n", h=HC), AX_X, ALU.max,
                                negate=True).then_inc(max_ready[h2], 1)

            def mask_and_sum(k, s, h2):
                n = G * k + s
                if s == 0:
                    dve.wait_ge(clip_ready, k + 1)
                dve.wait_ge(exp_ready[h2], n + 1)
                for h in range(h2 * HC, (h2 + 1) * HC):
                    last = v.scalar_tensor_tensor(probs[:, s % 2, h, :], probs[:, s % 2, h, :], 1.0,
                                                  adj_clip[:, s, :], ALU.mult, ALU.mult,
                                                  accum_out=sums[:, s % 2, h:h + 1])
                last.then_inc(sum_ready[h2], 1)
                hs = slice(h2 * HC, (h2 + 1) * HC)
                dve.wait_ge(sum_ready[h2], n + 1)
                v.reciprocal(rinv[:, s % 2, hs], sums[:, s % 2, hs]).then_inc(rinv_ready[h2], 1)

            def lower_ot(k, s):
                dve.wait_ge(ot_hi_ready, G * k + s + 1)
                v.tensor_tensor(OT[1][:, :, :], ot_ps[:, 0:C * N].rearrange("p (c n) -> p c n", c=C),
                                OT[0][:, :, :].bitcast(F32), ALU.subtract).then_inc(ot_copied, 1)

            def add_residual(k, s):
                n = G * k + s
                dve.wait_ge(y_filled, n + 1)
                if s == 0:
                    dve.wait_ge(resid_ready, k + 1)
                at_least(dve, scaled_ready, n - 1)
                v.tensor_tensor(y[:, s % 2, :], y_ps[:, 0:D], resid[:, s, :], ALU.add).then_inc(y_ready, 1)
                dve.wait_ge(y_ready, n + 1)
                v.bn_stats(stats[:, s % 2, :], y[:, s % 2, :]).then_inc(stats_ready, 1)

            def mean_variance(k, s):
                n = G * k + s
                wait_apart(dve, stats_ready, n + 1)
                v.bn_aggr(mean_var[:, s % 2, :], stats[:, s % 2, :]).then_inc(var_ready, 1)

            def iteration(t):
                if there(t):
                    row_max(t, 0, 1)
                if there(t - 1):
                    add_residual(t - 1, 1)
                if there(t):
                    mask_and_sum(t, 0, 1)
                if there(t - 1):
                    mean_variance(t - 1, 1)
                if there(t):
                    row_max(t, 0, 0)
                if there(t - 1):
                    lower_ot(t - 1, 2)
                if there(t + 1):
                    make_mask(t + 1)
                if there(t):
                    row_max(t, 1, 1)
                    mask_and_sum(t, 0, 0)
                if there(t + 1):
                    bias_q(t + 1)
                if there(t - 1):
                    add_residual(t - 1, 2)
                if there(t + 1):
                    make_logits(t + 1)
                if there(t - 1):
                    mean_variance(t - 1, 2)
                if there(t + 1):
                    max_logits(t + 1)
                if there(t - 1):
                    lower_ot(t - 1, 3)
                if there(t + 1):
                    leaky_relu(t + 1)
                    leaky_max(t + 1)
                if there(t):
                    row_max(t, 1, 0)
                if there(t - 1):
                    add_residual(t - 1, 3)
                if there(t):
                    row_max(t, 2, 1)
                    mask_and_sum(t, 1, 1)
                    mask_and_sum(t, 1, 0)
                if there(t + 1):
                    invert_sum0(t + 1)
                if there(t):
                    row_max(t, 2, 0)
                if there(t - 1):
                    mean_variance(t - 1, 3)
                if there(t + 1):
                    make_x1(t + 1, 0)
                    make_x1(t + 1, 1)
                if there(t):
                    mask_and_sum(t, 2, 0)
                if there(t + 1):
                    lower_x1T(t + 1, 0)
                    lower_x1T(t + 1, 1)
                if there(t):
                    row_max(t, 3, 0)
                    mask_and_sum(t, 2, 1)
                    row_max(t, 3, 1)
                    lower_ot(t, 0)
                if there(t + 1):
                    lower_k(t + 1, 1)
                if there(t):
                    mask_and_sum(t, 3, 0)
                if there(t + 1):
                    lower_q(t + 1, 1)
                if there(t):
                    add_residual(t, 0)
                if there(t + 1):
                    lower_k(t + 1, 0)
                if there(t):
                    mask_and_sum(t, 3, 1)
                    lower_ot(t, 1)
                    mean_variance(t, 0)
                if there(t + 1):
                    clip_adj(t + 1)
                    lower_q(t + 1, 0)

            dve.wait_ge(folded_loaded, 16 * len(FOLDED))
            dve.wait_ge(fold_filled, 1)
            v.tensor_copy(fcw_in[:, :, D:D + 2],
                          y_ps[:, 0:4].rearrange("p (c w) -> p c w", c=C)).then_inc(fold_copied, 1)
            v.tensor_tensor(qkb[:, :], y_ps[:, 4:6], qkb[:, :], ALU.add).then_inc(fold_copied, 1)
            dve.wait_ge(fold_copied, 2)
            v.tensor_tensor(logit_bias[:, :], qkb[:, 0:1], qkb[:, 1:2], ALU.add).then_inc(fold_copied, 1)
            dve.wait_ge(fcw_hi_ready, 1)
            v.tensor_tensor(fcw[1][:, :, :], fcw_in[:, :, :], fcw[0][:, :, :].bitcast(F32),
                            ALU.subtract).then_inc(weights_split, 1)
            dve.wait_ge(weights_loaded, 16 * len(WEIGHTS))
            dve.wait_ge(fold_filled, 2)
            v.tensor_tensor(bo_row[:, :], y_ps[:, 0:D], bo_row[:, :], ALU.add).then_inc(fold_copied, 1)
            dve.wait_ge(fold_copied, 4)
            dve.wait_ge(weights_hi, 5)
            for n, w in enumerate((wq, wk, wv, wo)):
                v.scalar_tensor_tensor(w[1][:, :, :], w_in[:, n, :, :], SCALE if n == 0 else 1.0,
                                       w[0][:, :, :].bitcast(F32), ALU.mult, ALU.subtract).then_inc(weights_split, 1)
            over_groups(dve, iteration)

        @block.gpsimd
        def _(pool):
            g_ = nc.gpsimd

            def lower_xT(u):
                pool.wait_ge(xT_hi_ready, u + 1)
                g_.tensor_tensor(xT_parts[1][:, :, :, :], xT_in[:, :, :, :], xT_parts[0][:, :, :, :].bitcast(F32),
                                 ALU.subtract).then_inc(xT_split, 1)

            def add_fc_bias(u):
                if not (isinstance(u, int) and u == 0):
                    pool.wait_ge(drained[LAST_AV], u)
                pool.wait_ge(x_loaded, 16 * (u + 1))
                g_.tensor_tensor(x_b[:, :, :], x_in[:, :, :], fcb[:, :].unsqueeze(1).to_broadcast([P, G, D]),
                                 ALU.add).then_inc(x_b_ready, 1)

            def add_out_bias(k):
                pool.wait_ge(drained[LAST_AV], k + 1)
                at_least(pool, y_ready, G * k)
                if isinstance(k, int) and k == 0:
                    pool.wait_ge(fold_copied, 4)
                g_.tensor_tensor(resid[:, :, :], x1[:, :, :], bo_row[:, :].unsqueeze(1).to_broadcast([P, G, D]),
                                 ALU.add).then_inc(resid_ready, 1)

            def scale_probs(k, s, h2):
                hs = slice(h2 * HC, (h2 + 1) * HC)
                pool.wait_ge(rinv_ready[h2], G * k + s + 1)
                g_.tensor_tensor(probs[:, s % 2, hs, :], probs[:, s % 2, hs, :],
                                 rinv[:, s % 2, hs].unsqueeze(2).to_broadcast([P, HC, N]),
                                 ALU.mult).then_inc(probs_ready[h2], 1)

            def inverse_deviation(k, s):
                n, i = G * k + s, s % 2
                pool.wait_ge(var_ready, n + 1)
                at_least(pool, scaled_ready, n - 1)
                g_.tensor_tensor(var_eps[:, i, :], mean_var[:, i, 1:2], eps_col[:, :], ALU.add).then_inc(eps_added, 1)
                g_.tensor_tensor(neg_mean[:, i, :], mean_var[:, i, 0:1], minus_one[:, :], ALU.mult)
                pool.wait_ge(eps_added, n + 1)
                g_.tensor_tensor(rstd[:, i, :], var_eps[:, i, :], halves[:, :], ALU.pow).then_inc(rstd_ready, 1)
                pool.wait_ge(rstd_ready, n + 1)
                g_.tensor_tensor(shift[:, i, :], neg_mean[:, i, :], rstd[:, i, :], ALU.mult).then_inc(shift_ready, 1)

            def apply_gamma_beta(k, s):
                n, i = G * k + s, s % 2
                pool.wait_ge(scaled_ready, n + 1)
                at_least(pool, out_ready, n - 1)
                g_.tensor_tensor(out_gamma[:, i, :], scaled[:, i, :], gamma_row[:, :], ALU.mult).then_inc(gamma_ready, 1)
                pool.wait_ge(gamma_ready, n + 1)
                at_least(pool, out_stored[s], 16 * k)
                g_.tensor_tensor(out_sb[:, s, :], out_gamma[:, i, :], beta_row[:, :], ALU.add).then_inc(out_ready, 1)

            def iteration(t):
                if there(t + 1):
                    lower_xT(t + 1)
                if there(t - 1):
                    inverse_deviation(t - 1, 0)
                    scale_probs(t - 1, 3, 1)
                if there(t + 1):
                    add_fc_bias(t + 1)
                if there(t):
                    scale_probs(t, 0, 1)
                if there(t - 1):
                    inverse_deviation(t - 1, 1)
                    apply_gamma_beta(t - 1, 0)
                    inverse_deviation(t - 1, 2)
                if there(t):
                    scale_probs(t, 0, 0)
                if there(t - 1):
                    apply_gamma_beta(t - 1, 1)
                if there(t):
                    add_out_bias(t)
                    scale_probs(t, 1, 0)
                    scale_probs(t, 1, 1)
                if there(t - 1):
                    apply_gamma_beta(t - 1, 2)
                    inverse_deviation(t - 1, 3)
                if there(t):
                    scale_probs(t, 2, 1)
                    scale_probs(t, 2, 0)
                if there(t - 1):
                    apply_gamma_beta(t - 1, 3)
                if there(t):
                    scale_probs(t, 3, 0)

            g_.memset(ident[:, :], 0.0).then_inc(ident_step, 1)
            g_.memset(halves[:, :], -0.5).then_inc(ident_step, 1)
            g_.memset(eps_col[:, :], EPS).then_inc(ident_step, 1)
            g_.memset(minus_one[:, :], -1.0).then_inc(ident_step, 1)
            pool.wait_ge(ident_step, 4)
            g_.affine_select(out=ident[:, :], in_=ident[:, :], compare_op=ALU.not_equal, fill=1.0, base=0,
                             pattern=[[-1, P]], channel_multiplier=1).then_inc(consts_ready, 1)
            g_.memset(KD[:, :, :, :, :, :].bitcast(F32), 0.0).then_inc(kd_zeroed, 1)
            pool.wait_ge(consts_ready, 1)
            pool.wait_ge(weights_loaded, 16 * len(WEIGHTS))
            over_groups(pool, iteration)


_INS = ["x", "xT", "adj", "fc_w", "fc_wT", "vectors", "qk_b", "wT", "row_vectors"]


def kernel(x, adj, L0_gnn_fc_w, L0_gnn_fc_b, L0_gnn_q_w, L0_gnn_q_b, L0_gnn_k_w, L0_gnn_k_b,
           L1_gnn_Wq, L1_gnn_bq, L1_gnn_Wk, L1_gnn_bk, L1_gnn_Wv, L1_gnn_bv, L1_gnn_Wo, L1_gnn_bo,
           L1_gnn_gamma, L1_gnn_beta):
    import numpy as np
    import concourse.bacc as bacc
    from concourse.bass_utils import run_bass_kernel_spmd

    columns = np.stack([np.reshape(v, D) for v in (L0_gnn_q_w, L0_gnn_k_w, L0_gnn_fc_b, L1_gnn_bq, L1_gnn_bk,
                                                    L1_gnn_bv)])
    given = dict(
        x=x, xT=np.transpose(np.asarray(x), (0, 2, 1)), adj=adj,
        fc_w=L0_gnn_fc_w, fc_wT=np.asarray(L0_gnn_fc_w).T,
        vectors=np.transpose(np.reshape(columns, (6, C, P)), (2, 1, 0)),
        qk_b=np.concatenate([np.reshape(L0_gnn_q_b, 1), np.reshape(L0_gnn_k_b, 1)]),
        wT=np.stack([np.asarray(w).T for w in (L1_gnn_Wq, L1_gnn_Wk, L1_gnn_Wv, L1_gnn_Wo)]),
        row_vectors=np.stack([L0_gnn_fc_b, L1_gnn_bo, L1_gnn_gamma, L1_gnn_beta]),
    )
    nc = bacc.Bacc("TRN2", target_bir_lowering=False, num_devices=1)
    arrays, args = {}, []
    for name in _INS:
        a = np.ascontiguousarray(given[name])
        arrays[f"in_{name}"] = a
        args.append(nc.dram_tensor(f"in_{name}", a.shape, mybir.dt.from_np(a.dtype), kind="ExternalInput").ap())
    out = nc.dram_tensor("out", (B, N, D), F32, kind="ExternalOutput").ap()
    gat_then_attention(nc, *args, out)
    r = run_bass_kernel_spmd(nc, [arrays], core_ids=[0])
    return r.results[0]["out"]
```
